# Optimizing a Trainium2 kernel written in Bass

```python
import numpy as np
import jax
import jax.numpy as jnp

def _softmax(x, axis=-1):
    return jax.nn.softmax(x, axis=axis)

def _gelu(x):
    return jax.nn.gelu(x, approximate=True)

def _silu(x):
    return jax.nn.silu(x)

def _sigmoid(x):
    return jax.nn.sigmoid(x)

def _layernorm(x, axis=-1, eps=1e-05):
    m = jnp.mean(x, axis=axis, keepdims=True)
    v = jnp.var(x, axis=axis, keepdims=True)
    return (x - m) / jnp.sqrt(v + eps)

def _scatter_add(tgt, idx, src, axis=0):
    return tgt.at[idx].add(src)

def _segment_sum(src, seg, n):
    return jax.ops.segment_sum(src, seg, n)
kernel_name = 'mk_decoder_preln_d1_seqx_r8_25c449'

def setup_inputs(seed: int=0):
    np.random.seed(seed)
    _w = jnp.asarray

    def _rec_inputs():
        import jax
        import jax.numpy as jnp
        _rk = jax.random.key(seed)
        x = -0.000125 + 0.9999 * jax.random.normal(jax.random.fold_in(_rk, 1), (64, 64, 128), jnp.float32)
        _lenS = 64 - jax.random.randint(jax.random.fold_in(_rk, 7), (64,), 0, max(1, 64 // 4) + 1, jnp.int32)
        _lenS2 = 64 - jax.random.randint(jax.random.fold_in(_rk, 8), (64,), 0, max(1, 64 // 4) + 1, jnp.int32)
        _ctx_1024P = jax.random.normal(jax.random.fold_in(_rk, 11), (64, 16, 128), jnp.float32)
        _ctx_1024c = jax.random.dirichlet(jax.random.fold_in(_rk, 511), 0.3 * jnp.ones((16,), jnp.float32), (64, 64))
        _ctx_1024t = jnp.einsum('bsk,bkd->bsd', _ctx_1024c, _ctx_1024P)
        _ctx_1024t = _ctx_1024t * jax.lax.rsqrt(jnp.mean(jnp.square(_ctx_1024t)) + 1e-12) * 0.953939
        ctx_1024 = -1.52775e-05 + 0.999936 * (_ctx_1024t + 0.3 * jax.random.normal(jax.random.fold_in(_rk, 611), (64, 64, 128), jnp.float32))
        return (x, ctx_1024)
    x, ctx_1024 = _rec_inputs()

    def _L0_attn_setup():
        import jax, jax.numpy as jnp
        import numpy as np
        D_MODEL = 128
        NUM_HEADS = 16
        DEPTH = D_MODEL // NUM_HEADS
        B, T = (2, 256)

        def _rope(x):
            H = x.shape[1]
            D = x.shape[-1]
            inv_freq = 1.0 / 10000.0 ** (jnp.arange(0, D, 2, dtype=jnp.float32) / D)
            freqs = jnp.arange(H, dtype=jnp.float32)[:, None] * inv_freq[None, :]
            sin = jnp.sin(freqs)[:, None, :]
            cos = jnp.cos(freqs)[:, None, :]
            x1 = x[..., ::2]
            x2 = x[..., 1::2]
            rot = jnp.stack([x1 * cos - x2 * sin, x1 * sin + x2 * cos], axis=-1)
            return rot.reshape(x.shape)
        key = jax.random.key(seed)
        k_x, k_wq, k_bq, k_wf, k_bf = jax.random.split(key, 5)
        lim_qkv = 1.0 / np.sqrt(D_MODEL)
        lim_fc = 1.0 / np.sqrt(D_MODEL)
        return {'x': jax.random.normal(k_x, (B, T, D_MODEL), dtype=jnp.float32), 'w_qkv': jax.random.uniform(k_wq, (D_MODEL, 3 * D_MODEL), jnp.float32, -lim_qkv, lim_qkv), 'b_qkv': jax.random.uniform(k_bq, (3 * D_MODEL,), jnp.float32, -lim_qkv, lim_qkv), 'w_fc': jax.random.uniform(k_wf, (D_MODEL, D_MODEL), jnp.float32, -lim_fc, lim_fc), 'b_fc': jax.random.uniform(k_bf, (D_MODEL,), jnp.float32, -lim_fc, lim_fc)}
    _L0_attn_all = _L0_attn_setup()
    _L0_attn_in = {k: v for k, v in _L0_attn_all.items() if k in ('w_qkv', 'b_qkv', 'w_fc', 'b_fc')}
    del _L0_attn_all

    def _L0_xattn_setup():
        import jax, jax.numpy as jnp
        import numpy as np
        DECAY = 0.9
        key = jax.random.key(seed)
        k1, k2, k3 = jax.random.split(key, 3)
        B, S, D = (8, 512, 128)
        q = jax.random.normal(k1, (B, S, D), dtype=jnp.float32)
        k = jax.random.normal(k2, (B, S, D), dtype=jnp.float32)
        v = jax.random.normal(k3, (B, S, D), dtype=jnp.float32)
        return {'q': q, 'k': k, 'v': v}
    _L0_xattn_all = _L0_xattn_setup()
    _L0_xattn_in = {k: v for k, v in _L0_xattn_all.items() if k in ()}
    del _L0_xattn_all

    def _L0_ffn_setup():
        import jax, jax.numpy as jnp
        import numpy as np
        B, S, H, E = (8, 512, 128, 8)
        TEMPERATURE = 1.0
        key = jax.random.key(seed)
        ks = jax.random.split(key, 7)
        s_h = 1.0 / np.sqrt(H).astype(np.float32)
        s_h2 = 1.0 / np.sqrt(H // 2).astype(np.float32)
        return {'hidden_states': jax.random.normal(ks[0], (B, S, H), jnp.float32), 'W1': jax.random.normal(ks[1], (H, H // 2), jnp.float32) * s_h, 'b1': jnp.zeros((H // 2,), jnp.float32), 'W2': jax.random.normal(ks[2], (H // 2, E), jnp.float32) * s_h2, 'b2': jnp.zeros((E,), jnp.float32), 'expert_W': jax.random.normal(ks[3], (E, H, H), jnp.float32) * s_h, 'expert_b': jax.random.normal(ks[4], (E, H), jnp.float32)}
    _L0_ffn_all = _L0_ffn_setup()
    _L0_ffn_in = {k: v for k, v in _L0_ffn_all.items() if k in ('W1', 'b1', 'W2', 'b2', 'expert_W', 'expert_b')}
    del _L0_ffn_all
    return {'x': x, 'ctx_1024': ctx_1024, 'L0_attn_w_qkv': _L0_attn_in['w_qkv'], 'L0_attn_b_qkv': _L0_attn_in['b_qkv'], 'L0_attn_w_fc': _L0_attn_in['w_fc'], 'L0_attn_b_fc': _L0_attn_in['b_fc'], 'L0_ffn_W1': _L0_ffn_in['W1'], 'L0_ffn_b1': _L0_ffn_in['b1'], 'L0_ffn_W2': _L0_ffn_in['W2'], 'L0_ffn_b2': _L0_ffn_in['b2'], 'L0_ffn_expert_W': _L0_ffn_in['expert_W'], 'L0_ffn_expert_b': _L0_ffn_in['expert_b']}

def reference(x, ctx_1024, L0_attn_w_qkv, L0_attn_b_qkv, L0_attn_w_fc, L0_attn_b_fc, L0_ffn_W1, L0_ffn_b1, L0_ffn_W2, L0_ffn_b2, L0_ffn_expert_W, L0_ffn_expert_b):
    import jax
    import jax.numpy as jnp

    def _L0_attn_ref(x, w_qkv, b_qkv, w_fc, b_fc):
        import jax, jax.numpy as jnp
        import numpy as np
        D_MODEL = 128
        NUM_HEADS = 16
        DEPTH = D_MODEL // NUM_HEADS
        B, T = (2, 256)

        def _rope(x):
            H = x.shape[1]
            D = x.shape[-1]
            inv_freq = 1.0 / 10000.0 ** (jnp.arange(0, D, 2, dtype=jnp.float32) / D)
            freqs = jnp.arange(H, dtype=jnp.float32)[:, None] * inv_freq[None, :]
            sin = jnp.sin(freqs)[:, None, :]
            cos = jnp.cos(freqs)[:, None, :]
            x1 = x[..., ::2]
            x2 = x[..., 1::2]
            rot = jnp.stack([x1 * cos - x2 * sin, x1 * sin + x2 * cos], axis=-1)
            return rot.reshape(x.shape)
        Bs, Ts, C = x.shape
        H, D = (NUM_HEADS, DEPTH)
        qkv = x @ w_qkv + b_qkv
        qkv = qkv.reshape(Bs, Ts, 3, H, D)
        qkv = jnp.transpose(qkv, (2, 0, 3, 1, 4))
        q, k, v = (qkv[0], qkv[1], qkv[2])
        q = _rope(q)
        k = _rope(k)
        scores = jnp.einsum('bhtd,bhsd->bhts', q, k) / jnp.sqrt(jnp.float32(D))
        attn = jax.nn.softmax(scores, axis=-1)
        out = jnp.einsum('bhts,bhsd->bhtd', attn, v)
        out = jnp.transpose(out, (0, 2, 1, 3)).reshape(Bs, Ts, C)
        return out @ w_fc + b_fc

    def _L0_xattn_ref(q, k, v):
        import jax, jax.numpy as jnp
        import numpy as np
        DECAY = 0.9
        kv = jnp.swapaxes(k * v, 0, 1)

        def step(r, kv_t):
            r = DECAY * r + kv_t
            return (r, r)
        r0 = jnp.zeros(q.shape[:1] + q.shape[2:], dtype=q.dtype)
        _, rs = jax.lax.scan(step, r0, kv)
        return q * jnp.swapaxes(rs, 0, 1)

    def _L0_ffn_ref(hidden_states, W1, b1, W2, b2, expert_W, expert_b):
        import jax, jax.numpy as jnp
        import numpy as np
        B, S, H, E = (8, 512, 128, 8)
        TEMPERATURE = 1.0
        h = jax.nn.relu(jnp.einsum('bsh,hf->bsf', hidden_states, W1) + b1)
        logits = jnp.einsum('bsf,fe->bse', h, W2) + b2
        probs = jax.nn.softmax(logits / TEMPERATURE, axis=-1)
        sel = jnp.argmax(probs, axis=-1)
        out = jnp.zeros_like(hidden_states)
        for e in range(E):
            mask = (sel == e)[..., None].astype(hidden_states.dtype)
            xe = hidden_states * mask
            ye = jnp.einsum('bsh,hd->bsd', xe, expert_W[e]) + expert_b[e]
            out = out + ye * mask
        return out
    x = x + _L0_attn_ref(_layernorm(x, axis=-1), L0_attn_w_qkv, L0_attn_b_qkv, L0_attn_w_fc, L0_attn_b_fc)
    x = x + _L0_xattn_ref(_layernorm(x, axis=-1), ctx_1024, ctx_1024)
    x = x + _L0_ffn_ref(_layernorm(x, axis=-1), L0_ffn_W1, L0_ffn_b1, L0_ffn_W2, L0_ffn_b2, L0_ffn_expert_W, L0_ffn_expert_b)
    return x

_drawn_inputs = setup_inputs


def setup_inputs(seed=0):
    import zlib

    import numpy as np

    out = dict(_drawn_inputs(seed))
    spreads = {'L0_ffn_b1': (0.0, 0.1), 'L0_ffn_b2': (0.0, 0.1)}
    factors = {}
    for name, (base, spread) in spreads.items():
        noise = np.random.default_rng([zlib.crc32(name.encode()), seed]).standard_normal(out[name].shape)
        drawn = base * np.exp(spread * noise) if base else spread * noise
        out[name] = jnp.asarray(drawn.astype(out[name].dtype))
    for name, factor in factors.items():
        out[name] = (out[name] * factor).astype(out[name].dtype)
    return out
```

```python
from contextlib import ExitStack

import numpy as np

import concourse.bass as bass
from concourse import mybir

ALU = mybir.AluOpType
ACT = mybir.ActivationFunctionType
F32 = mybir.dt.float32
F16 = mybir.dt.float16
BF16 = mybir.dt.bfloat16
AX_X = mybir.AxisListType.X

P = 128
T = 64
HEADS = 16
DEPTH = 8
QUADS = 4
EXPERTS = 8
HIDDEN = 64
RING = 4
EPS = 1e-5
SCALE = float(DEPTH) ** -0.5
VCOL = 2 * 2 * (DEPTH + 1)
VSTREAM = 96
PARTS = 3


def decoder_layer(nc, x, ctx_in, w_qkv, b_qkv, w_fc, b_fc, w1, b1, w2, b2, ew, eb, rope, ident, decay, first, out):
    tiles = x.shape[0] * x.shape[1] // P
    x_t = x.rearrange("(n b) t d -> n (b t) d", b=2)
    ctx_t = ctx_in.rearrange("(n b) t d -> n (b t) d", b=2)
    out_t = out.rearrange("(n b) t d -> n (b t) d", b=2)

    with ExitStack() as stack:
        def sb(name, shape, dt=F32):
            return stack.enter_context(nc.sbuf_tensor(name, shape, dt))

        def sem(name):
            return stack.enter_context(nc.semaphore(name))

        w_all = sb("w_all", [P, 3 * P])
        w_qk = sb("w_qk", [P, 2 * P])
        w_v = sb("w_v", [P, P])
        rot = sb("rot", [P, 4, P])
        b_all = sb("b_all", [1, 3 * P])
        b_rot = sb("b_rot", [1, 3 * P])
        rotb = sb("rotb", [1, 4, P])
        rope_sb = sb("rope_sb", [P, 2, P])
        bres = sb("bres", [1, 2, 4 * P])
        bias_part = sb("bias_part", [1, PARTS, 4 * P], BF16)
        bias_rows = sb("bias_rows", [PARTS, 4 * P], BF16)
        ones_rows = sb("ones_rows", [PARTS, P], BF16)
        b_fc_sb = sb("b_fc_sb", [1, P])
        wfc = sb("wfc", [P, P])
        w1_sb = sb("w1_sb", [P, HIDDEN])
        b1_sb = sb("b1_sb", [HIDDEN, 1])
        w2_sb = sb("w2_sb", [HIDDEN, EXPERTS])
        b2_sb = sb("b2_sb", [P, EXPERTS])
        first_sb = sb("first_sb", [P, EXPERTS])
        ew_sb = sb("ew_sb", [P, EXPERTS, P])
        eb_sb = sb("eb_sb", [PARTS * EXPERTS, P])
        ebr = sb("ebr", [PARTS * EXPERTS, 2, P])
        ebp = sb("ebp", [PARTS * EXPERTS, PARTS, P], BF16)
        eb_rows = sb("eb_rows", [PARTS * EXPERTS, P], BF16)
        id32 = sb("id32", [P, P])
        id16 = sb("id16", [P, P], F16)
        idb = sb("idb", [P, P], BF16)
        neg_id = sb("neg_id", [P, P], BF16)
        decay_sb = sb("decay_sb", [P, P])
        eps_sb = sb("eps_sb", [P, 1])
        half = sb("half", [P, 1])

        X = sb("X", [P, RING, P])
        C = sb("C", [P, RING, P])
        st = sb("st", [P, 3, 6])
        mv = sb("mv", [P, 3, 2, 2])
        ve = sb("ve", [P, 3, 1])
        rstd = sb("rstd", [P, 3, 2, 1])
        xn1 = sb("xn1", [P, 2, P])
        xT = sb("xT", [P, 2, P])
        parts = sb("parts", [P, 2, 2, HEADS, 4, DEPTH], F16)
        qkT = sb("qkT", [P, 2, 2, QUADS, P], F16)
        V = sb("V", [P, RING, 7 * VCOL + VSTREAM])
        mx = sb("mx", [P, 2, HEADS])
        mhi = sb("mhi", [P, 2, HEADS], BF16)
        mlo = sb("mlo", [P, 2, HEADS], BF16)
        E = sb("E", [P, 2, 2 * 512])
        ET = sb("ET", [P, 2, 8, P])
        rec = sb("rec", [P, HEADS])
        att = sb("att", [P, P])
        attT = sb("attT", [P, P])
        x1 = sb("x1", [P, 2, P])
        kv = sb("kv", [P, 2, P])
        gated = sb("gated", [P, P])
        x2 = sb("x2", [P, RING, P])
        xn3 = sb("xn3", [P, 2, P])
        x3T = sb("x3T", [P, 2, P])
        hT = sb("hT", [HIDDEN, P])
        lg = sb("lg", [P, EXPERTS])
        top = sb("top", [P, 2])
        pick = sb("pick", [P, EXPERTS])
        mask = sb("mask", [P, 2, PARTS, EXPERTS], BF16)
        maskT = sb("maskT", [PARTS * EXPERTS, P], BF16)
        xm = sb("xm", [P, EXPERTS, P])
        O = sb("O", [P, RING, P])

        ps_s = stack.enter_context(nc.psum_tensor("ps_s", [P, 2, 512], F32))
        ps_t = stack.enter_context(nc.psum_tensor("ps_t", [P, 2, 512], F32))
        ps_p = stack.enter_context(nc.psum_tensor("ps_p", [P, 512], F32))
        ps_q = stack.enter_context(nc.psum_tensor("ps_q", [P, 1024], F16))
        ps_c = stack.enter_context(nc.psum_tensor("ps_c", [P, 512], F32))
        ps_d = stack.enter_context(nc.psum_tensor("ps_d", [P, 512], F32))
        ps_v = ps_q[:, 0:2 * P].bitcast(F32)

        x_in = [sem(f"x_in{u}") for u in range(RING)]
        c_in = [sem(f"c_in{u}") for u in range(RING)]
        o_out = [sem(f"o_out{u}") for u in range(RING)]
        w_in = sem("w_in")
        setup = sem("setup")
        pool_setup = sem("pool_setup")
        rows_in = sem("rows_in")
        names = ("st1 mv1 ve1 rstd1 xn1 xT_ps xT s_0 s_2 s_1 qk_ps v_ps hi lo_q lo_k dup_q dup_k v_up v_down qkT_ps qkT s_ps mx mhi mlo sm_ps "
                 "exp eT_ps eT_a eT_b pv_ps rec_a rec_b att_a att_b attT_ps attT kv rs_ps x1 st2 mv2 ve2 rstd2 "
                 "gated x2 st3 mv3 ve3 rstd3 xn3 x3T_ps x3T h_ps hT lg_ps lg top1 pick top2 mask maskT_ps maskT "
                 "mask_ps xm y_ps o").split()
        S = {n: sem("s_" + n) for n in names}

        def done(eng, name, t):
            if isinstance(t, int) and t < 0:
                return
            eng.wait_ge(S[name], t + 1)

        def has(t):
            return not isinstance(t, int) or 0 <= t < tiles

        def steps(eng, step):
            begin, end = 2 * RING, (tiles - 1) // RING * RING
            for s in range(-1, begin):
                step(s, s % RING)
            with eng.Fori(begin, end, RING) as s0:
                for u in range(RING):
                    step(s0 + u, u)
            for s in range(end, tiles + 4):
                step(s, s % RING)

        def ring_count(t, u, off):
            slot = (u - off) % RING
            if isinstance(t, int):
                return 16 * (t // RING + 1)
            return (t - slot) * (16 // RING) + 16

        weights = [
            (w_all[:, :], w_qkv), (b_all[:, :], b_qkv.rearrange("(a n) -> a n", a=1)),
            (rope_sb[:, :, :], rope.rearrange("(a c) n -> a c n", a=1).to_broadcast([P, 2, P])),
            (id32[:, :], ident), (b_fc_sb[:, :], b_fc.rearrange("(a n) -> a n", a=1)),
            (decay_sb[:, :], decay), (w1_sb[:, :], w1), (b1_sb[:, :], b1.rearrange("(n a) -> n a", a=1)),
            (w2_sb[:, :], w2), (b2_sb[:, :], b2.rearrange("(a n) -> a n", a=1).to_broadcast([P, EXPERTS])),
            (first_sb[:, :], first.rearrange("(a n) -> a n", a=1).to_broadcast([P, EXPERTS])),
        ]
        fc_rows = w_fc.rearrange("(g j d) n -> j g d n", j=4, d=DEPTH)
        weights += [(wfc[32 * j:32 * j + 32, :], fc_rows[j]) for j in range(4)]
        weights += [(eb_sb[EXPERTS * c:EXPERTS * c + EXPERTS, :], eb) for c in range(PARTS)]
        weights += [(ew_sb[:, :, :], ew.rearrange("e k n -> k e n"))]
        W_ALL = 16 * len(weights)
        MOVES = 2 * PARTS
        SETUP = 2 + 2 * RING + 4 + 12 + 4 + 15

        block = stack.enter_context(nc.Block())

        @block.sync
        def _(sp):
            def step(s, u):
                z, o = s + 1, s - 4
                if has(z) and not (isinstance(z, int) and z < RING):
                    done(sp, "x1", z - RING)
                    sp.dma_start(X[:, z_slot(u), :], x_t[bass.ds(z, 1)].rearrange("a p d -> p (a d)")).then_inc(
                        x_in[z_slot(u)], 16)
                    done(sp, "kv", z - RING)
                    sp.dma_start(C[:, z_slot(u), :], ctx_t[bass.ds(z, 1)].rearrange("a p d -> p (a d)")).then_inc(
                        c_in[z_slot(u)], 16)
                if has(o):
                    done(sp, "o", o)
                    sp.dma_start(out_t[bass.ds(o, 1)].rearrange("a p d -> p (a d)"), O[:, u, :]).then_inc(
                        o_out[u], 16)

            def z_slot(u):
                return (u + 1) % RING

            sp.dma_start(X[:, 0, :], x_t[0]).then_inc(x_in[0], 16)
            for dst, src in weights[:4]:
                sp.dma_start(dst, src).then_inc(w_in, 16)
            for t in range(1, RING):
                sp.dma_start(X[:, t, :], x_t[t]).then_inc(x_in[t], 16)
            for dst, src in weights[4:]:
                sp.dma_start(dst, src).then_inc(w_in, 16)
            for t in range(RING):
                sp.dma_start(C[:, t, :], ctx_t[t]).then_inc(c_in[t], 16)
            sp.wait_ge(setup, SETUP)
            for c in range(PARTS):
                sp.dma_start(bias_rows[c:c + 1, :], bias_part[0:1, c, :]).then_inc(rows_in, 16)
                sp.dma_start(eb_rows[EXPERTS * c:EXPERTS * c + EXPERTS, :], ebp[0:EXPERTS, c, :]).then_inc(rows_in, 16)
            steps(sp, step)
            for u in range(RING):
                sp.wait_ge(o_out[u], 16 * (tiles // RING))

        @block.gpsimd
        def _(pool):
            nc.gpsimd.memset(half[:, :], -0.5).then_inc(pool_setup, 1)
            nc.gpsimd.memset(eps_sb[:, :], EPS).then_inc(pool_setup, 1)
            pool.wait_ge(pool_setup, 2)

            def step(s, u):
                z, a, c = s + 1, s, s - 2
                p_z, p_a, p_c = (u + 1) % 2, u % 2, u % 2

                def root(n, t, p):
                    done(pool, f"mv{n}", t)
                    nc.gpsimd.tensor_tensor(ve[:, n - 1, :], mv[:, n - 1, p, 1:2], eps_sb[:, :],
                                            ALU.add).then_inc(S[f"ve{n}"], 1)
                    done(pool, f"ve{n}", t)
                    nc.gpsimd.tensor_tensor(rstd[:, n - 1, p, :], ve[:, n - 1, :], half[:, :],
                                            ALU.pow).then_inc(S[f"rstd{n}"], 1)

                if has(z):
                    root(1, z, p_z)
                if has(c):
                    pool.wait_ge(c_in[(u - 2) % RING], ring_count(c, u, 2))
                    done(pool, "rs_ps", c - 2)
                    cc = C[:, (u - 2) % RING, :]
                    nc.gpsimd.tensor_tensor(kv[:, p_c, :], cc, cc, ALU.mult).then_inc(S["kv"], 1)
                if has(c):
                    root(2, c, p_c)
                    root(3, c, p_c)

            steps(pool, step)

        @block.vector
        def _(dve):
            v = nc.vector
            count = 0

            def link(ins):
                nonlocal count
                count += 1
                ins.then_inc(setup, 1)
                dve.wait_ge(setup, count)

            for slot in range(2):
                link(v.memset(V[:, 2 * slot:2 * slot + 2, :], 0.0))
            for half_ in range(2):
                ones = V[64 * half_:64 * half_ + 64, :, 0:8 * VCOL].rearrange(
                    "p r (g b h f) -> p r g b h f", b=2, h=2, f=DEPTH + 1)
                for r in range(RING):
                    i = v.memset(ones[:, r, :, :, half_, DEPTH], 1.0)
                    if r < RING - 1:
                        i.then_inc(setup, 1)
                        count += 1
                    else:
                        link(i)
            link(v.memset(ones_rows[:, :], 1.0))
            dve.wait_ge(w_in, W_ALL)
            link(v.tensor_copy(id16[:, :], id32[:, :]))
            link(v.tensor_copy(idb[:, :], id32[:, :]))
            link(v.tensor_scalar(neg_id[:, :], id32[:, :], -1.0, None, ALU.mult))
            w_pairs = w_all[:, 0:2 * P].rearrange("p (m e) -> p e m", e=2)
            r_pairs = w_qk[:, :].rearrange("p (m e) -> p e m", e=2)
            b_pairs = b_all[:, 0:2 * P].rearrange("p (m e) -> p e m", e=2)
            br_pairs = b_rot[:, 0:2 * P].rearrange("p (m e) -> p e m", e=2)
            for src, dst, r, n in ((w_pairs, r_pairs, rot, P), (b_pairs, br_pairs, rotb, 1)):
                for q, (e, cs) in enumerate(((0, 0), (1, 1), (0, 1), (1, 0))):
                    link(v.tensor_tensor(r[:, q, :], src[:, e, :], rope_sb[0:n, cs, :], ALU.mult))
                link(v.tensor_tensor(dst[:, 0, :], r[:, 0, :], r[:, 1, :], ALU.subtract))
                link(v.tensor_tensor(dst[:, 1, :], r[:, 2, :], r[:, 3, :], ALU.add))
            for h2 in range(2):
                for src, dst in ((w_all[:, 2 * P:], w_v[:, :]), (b_all[:, 2 * P:], b_rot[:, 2 * P:])):
                    s_ = src.rearrange("p (g h j d) -> p h j g d", g=2, h=2, j=4)[:, h2]
                    d_ = dst.rearrange("p (h j g d) -> p h j g d", g=2, h=2, j=4)[:, h2]
                    link(v.tensor_copy(d_, s_))
            def split(whole, res, part):
                link(v.tensor_copy(part(0), whole))
                link(v.tensor_tensor(res(0), whole, part(0), ALU.subtract))
                link(v.tensor_copy(part(1), res(0)))
                link(v.tensor_tensor(res(1), res(0), part(1), ALU.subtract))
                link(v.tensor_copy(part(2), res(1)))
            split(b_rot[:, :], lambda i: bres[:, i, 0:3 * P], lambda i: bias_part[:, i, 0:3 * P])
            split(b_fc_sb[:, :], lambda i: bres[:, i, 3 * P:], lambda i: bias_part[:, i, 3 * P:])
            split(eb_sb[:, :], lambda i: ebr[:, i, :], lambda i: ebp[:, i, :])
            assert count == SETUP, count

            def step(s, u):
                z, a, b, c, d, o = s + 1, s, s - 1, s - 2, s - 3, s - 4
                p_z, p_a, p_b, p_c, p_d = (u + 1) % 2, u % 2, (u + 1) % 2, u % 2, (u + 1) % 2

                def stats(n, t, p, src):
                    v.bn_stats(st[:, n - 1, :], src).then_inc(S[f"st{n}"], 1)
                    done(dve, f"st{n}", t)
                    dve.nop(nofuse=True)
                    v.bn_aggr(mv[:, n - 1, p, :], st[:, n - 1, :]).then_inc(S[f"mv{n}"], 1)

                if has(o):
                    done(dve, "y_ps", o)
                    if not isinstance(o, int):
                        dve.wait_ge(o_out[u], (o - u) * (16 // RING))
                    elif o >= RING:
                        dve.wait_ge(o_out[u], 16 * (o // RING))
                    v.tensor_tensor(O[:, u, :], ps_d[:, 0:P], x2[:, u, :], ALU.add).then_inc(S["o"], 1)
                if has(z):
                    dve.wait_ge(x_in[(u + 1) % RING], ring_count(z, u, -1))
                    stats(1, z, p_z, X[:, (u + 1) % RING, :])
                if has(b):
                    done(dve, "s_ps", b)
                    v.tensor_reduce(mx[:, p_b, :], ps_s[:, :, :].rearrange("p k (h t) -> p (k h) t", t=T), AX_X,
                                    ALU.max).then_inc(S["mx"], 1)
                    done(dve, "mx", b)
                    v.tensor_copy(mhi[:, p_b, :], mx[:, p_b, :]).then_inc(S["mhi"], 1)
                    done(dve, "mhi", b)
                    v.tensor_tensor(mlo[:, p_b, :], mx[:, p_b, :], mhi[:, p_b, :], ALU.subtract).then_inc(S["mlo"], 1)
                if has(z):
                    done(dve, "rstd1", z)
                    v.tensor_scalar(xn1[:, p_z, :], X[:, (u + 1) % RING, :], mv[:, 0, p_z, 0:1], rstd[:, 0, p_z, :],
                                    ALU.subtract, ALU.mult).then_inc(S["xn1"], 1)
                if has(c):
                    done(dve, "pv_ps", c)
                    done(dve, "attT_ps", c - 1)
                    for row, (r_name, a_name) in enumerate((("rec_a", "att_a"), ("rec_b", "att_b"))):
                        lo, hi = T * row, T * row + T
                        got = ps_c[lo:hi, 0:8 * VCOL].rearrange("p (g b h f) -> p b g h f", b=2, h=2,
                                                                f=DEPTH + 1)[:, row]
                        v.reciprocal(rec[lo:hi, :].rearrange("p (g h) -> p g h", h=2),
                                     got[:, :, :, DEPTH]).then_inc(S[r_name], 1)
                        done(dve, r_name, c)
                        v.tensor_tensor(
                            att[lo:hi, :].rearrange("p (g h f) -> p g h f", h=2, f=DEPTH), got[:, :, :, 0:DEPTH],
                            rec[lo:hi, :].rearrange("p (g h) -> p g h", h=2).unsqueeze(3).to_broadcast(
                                [T, 8, 2, DEPTH]), ALU.mult).then_inc(S[a_name], 1)
                if has(a):
                    done(dve, "qk_ps", a)
                    done(dve, "hi", a)
                    for qk, (lo, dup) in enumerate((("lo_q", "dup_q"), ("lo_k", "dup_k"))):
                        mine = parts[:, p_a, qk]
                        v.tensor_tensor(mine[:, :, 2 - qk, :],
                                        ps_p[:, P * qk:P * qk + P].rearrange("p (h d) -> p h d", d=DEPTH),
                                        mine[:, :, 0, :], ALU.subtract).then_inc(S[lo], 1)
                    done(dve, "lo_q", a)
                    pairs = parts[:, p_a, 0].rearrange("p h (a c) d -> p h c a d", c=2)
                    v.tensor_copy(pairs[:, :, 1], pairs[:, :, 0]).then_inc(S["dup_q"], 1)
                    done(dve, "lo_k", a)
                    v.tensor_copy(parts[:, p_a, 1, :, 2:4, :], parts[:, p_a, 1, :, 0:2, :]).then_inc(S["dup_k"], 1)
                if has(d):
                    done(dve, "lg_ps", d)
                    v.tensor_tensor(lg[:, :], ps_d[:, 384:384 + EXPERTS], b2_sb[:, :], ALU.add).then_inc(S["lg"], 1)
                    done(dve, "lg", d)
                    v.tensor_reduce(top[:, 0:1], lg[:, :], AX_X, ALU.max).then_inc(S["top1"], 1)
                    done(dve, "top1", d)
                    v.scalar_tensor_tensor(out=pick[:, :], in0=lg[:, :], scalar=top[:, 0:1], in1=first_sb[:, :],
                                           op0=ALU.is_ge, op1=ALU.mult).then_inc(S["pick"], 1)
                    done(dve, "pick", d)
                    v.tensor_reduce(top[:, 1:2], pick[:, :], AX_X, ALU.max).then_inc(S["top2"], 1)
                    done(dve, "top2", d)
                    v.tensor_scalar(mask[:, p_d, :, :], pick[:, :].unsqueeze(1).to_broadcast([P, PARTS, EXPERTS]), top[:, 1:2], None, ALU.is_equal).then_inc(S["mask"], 1)
                if has(c):
                    done(dve, "rs_ps", c)
                    v.tensor_tensor(x1[:, p_c, :], ps_c[:, P:2 * P], X[:, (u - 2) % RING, :], ALU.add).then_inc(S["x1"], 1)
                    done(dve, "x1", c)
                    stats(2, c, p_c, x1[:, p_c, :])
                if has(d):
                    done(dve, "mask_ps", d)
                    done(dve, "x3T", d)
                    done(dve, "y_ps", d - 1)
                    v.tensor_tensor(xm[:, :, :], x3T[:, p_d, :].unsqueeze(1).to_broadcast([P, EXPERTS, P]),
                                    ps_t[:, :, :].rearrange("p k (e t) -> p (k e) t", t=P),
                                    ALU.mult).then_inc(S["xm"], 1)
                if has(c):
                    done(dve, "rs_ps", c)
                    done(dve, "mv2", c)
                    v.scalar_tensor_tensor(out=gated[:, :], in0=x1[:, p_c, :], scalar=mv[:, 1, p_c, 0:1],
                                           in1=ps_c[:, 2 * P:3 * P], op0=ALU.subtract,
                                           op1=ALU.mult).then_inc(S["gated"], 1)
                    done(dve, "gated", c)
                    done(dve, "rstd2", c)
                    v.scalar_tensor_tensor(out=x2[:, (u - 2) % RING, :], in0=gated[:, :], scalar=rstd[:, 1, p_c, :],
                                           in1=x1[:, p_c, :], op0=ALU.mult, op1=ALU.add).then_inc(S["x2"], 1)
                    done(dve, "x2", c)
                    stats(3, c, p_c, x2[:, (u - 2) % RING, :])
                if has(a):
                    done(dve, "qkT_ps", a)
                    done(dve, "s_ps", a - 2)
                    v.tensor_copy(qkT[:, p_a, :, :, :].rearrange("p q g t -> p (q g t)"), ps_q[:, :]).then_inc(S["qkT"], 1)
                if has(c):
                    done(dve, "rstd3", c)
                    v.tensor_scalar(xn3[:, p_c, :], x2[:, (u - 2) % RING, :], mv[:, 2, p_c, 0:1], rstd[:, 2, p_c, :],
                                    ALU.subtract, ALU.mult).then_inc(S["xn3"], 1)
                if has(b):
                    done(dve, "eT_ps", b)
                    done(dve, "pv_ps", b - 2)
                    v.tensor_copy(ET[:, p_b, 4:8, :].rearrange("p g t -> p (g t)"), ps_t[:, 1, :]).then_inc(S["eT_b"], 1)

            steps(dve, step)

        @block.scalar
        def _(act):
            sc = nc.scalar

            def step(s, u):
                a, b, c, d = s, s - 1, s - 2, s - 3
                p_a, p_b, p_c, p_d = u % 2, (u + 1) % 2, u % 2, (u + 1) % 2
                if has(a):
                    done(act, "xT_ps", a)
                    done(act, "v_ps", a - 2)
                    sc.copy(xT[:, p_a, :], ps_p[:, 0:P]).then_inc(S["xT"], 1)
                if has(d):
                    done(act, "x3T_ps", d)
                    done(act, "h_ps", d - 2)
                    done(act, "xm", d - 2)
                    sc.copy(x3T[:, p_d, :], ps_d[:, P:2 * P]).then_inc(S["x3T"], 1)
                if has(a):
                    done(act, "qk_ps", a)
                    done(act, "qkT_ps", a - 2)
                    sc.copy(parts[:, p_a, :, :, 0, :].rearrange("p q h d -> p (q h) d"),
                            ps_p[:, 0:2 * P].rearrange("p (h d) -> p h d", d=DEPTH)).then_inc(S["hi"], 1)
                    done(act, "v_ps", a)
                    done(act, "pv_ps", a - RING)
                    for h2, name in ((0, "v_up"), (1, "v_down")):
                        src = ps_v[64 * h2:64 * h2 + 64, :].rearrange("p (b g d) -> p b g d", b=2, d=DEPTH)
                        dst = V[64 * h2:64 * h2 + 64, u, 0:8 * VCOL].rearrange(
                            "p (g b h f) -> p h b g f", b=2, h=2, f=DEPTH + 1)[:, h2, :, :, 0:DEPTH]
                        sc.copy(dst, src).then_inc(S[name], 1)
                if has(b):
                    done(act, "sm_ps", b)
                    done(act, "eT_ps", b - 2)
                    sc.activation(E[:, p_b, :], ps_s[:, :, :].rearrange("p k n -> p (k n)"), ACT.Exp,
                                  scale=SCALE).then_inc(S["exp"], 1)
                if has(d):
                    done(act, "h_ps", d)
                    done(act, "lg_ps", d - 1)
                    sc.activation(hT[:, :], ps_d[0:HIDDEN, 2 * P:3 * P], ACT.Relu, bias=b1_sb[:, :]).then_inc(S["hT"], 1)
                if has(c):
                    done(act, "attT_ps", c)
                    done(act, "rs_ps", c - 1)
                    sc.copy(attT[:, :], ps_c[:, 0:P]).then_inc(S["attT"], 1)
                if has(d):
                    done(act, "maskT_ps", d)
                    done(act, "y_ps", d - 1)
                    sc.copy(maskT[:, :], ps_d[0:PARTS * EXPERTS, 448:512].bitcast(BF16)).then_inc(S["maskT"], 1)
                if has(b):
                    done(act, "eT_ps", b)
                    done(act, "pv_ps", b - 2)
                    sc.copy(ET[:, p_b, 0:4, :].rearrange("p g t -> p (g t)"), ps_t[:, 0, :]).then_inc(S["eT_a"], 1)

            act.wait_ge(w_in, W_ALL)
            steps(act, step)

        @block.tensor
        def _(pe):
            mm = nc.tensor.matmul

            def step(s, u):
                a, b, c, d = s, s - 1, s - 2, s - 3
                p_a, p_b, p_c, p_d = u % 2, (u + 1) % 2, u % 2, (u + 1) % 2
                if has(b):
                    done(pe, "qkT", b)
                    done(pe, "exp", b - 1)
                    for j in (0, 2, 1, 3):
                        rows = slice(32 * j, 32 * j + 32)
                        if j % 2:
                            done(pe, f"s_{j - 1}", b)
                        for g in range(QUADS):
                            for row in range(2):
                                t = slice(T * row, T * row + T)
                                at = 256 * (j % 2) + 64 * g
                                last = mm(ps_s[t, j // 2, at:at + T], qkT[rows, p_b, 0, g, t], qkT[rows, p_b, 1, g, t],
                                          start=(j in (0, 2) and g == 0), stop=False, skip_group_check=True)
                        if j < 3:
                            last.then_inc(S[f"s_{j}"], 1)
                    last.then_inc(S["s_ps"], 1)
                if has(a):
                    done(pe, "xn1", a)
                    done(pe, "lo_k", a - 1)
                    nc.tensor.transpose(ps_p[:, 0:P], xn1[:, p_a, :], id32[:, :]).then_inc(S["xT_ps"], 1)
                if has(d):
                    done(pe, "xn3", d)
                    done(pe, "o", d - 1)
                    nc.tensor.transpose(ps_d[:, P:2 * P], xn3[:, p_d, :], id32[:, :]).then_inc(S["x3T_ps"], 1)
                if has(c):
                    done(pe, "eT_a", c)
                    done(pe, "eT_b", c)
                    done(pe, "v_down", c)
                    done(pe, "gated", c - 1)
                    for g in range(8):
                        last = mm(ps_c[:, VCOL * g:VCOL * g + VSTREAM], ET[:, p_c, g, :],
                                  V[:, (u - 2) % RING, VCOL * g:VCOL * g + VSTREAM], start=True, stop=True)
                    last.then_inc(S["pv_ps"], 1)
                if has(a):
                    done(pe, "xT", a)
                    mm(ps_p[:, 0:2 * P], xT[:, p_a, :], w_qk[:, :], start=True, stop=False)
                    mm(ps_p[:, 0:2 * P], ones_rows[:, :], bias_rows[:, 0:2 * P], start=False,
                       stop=True).then_inc(S["qk_ps"], 1)
                    done(pe, "qkT", a - 1)
                    for row in range(2):
                        for h2 in range(2):
                            dst = ps_v[T * h2:T * h2 + T, T * row:T * row + T]
                            mm(dst, xT[:, p_a, T * row:T * row + T], w_v[:, 64 * h2:64 * h2 + 64], start=True,
                               stop=False)
                            last = mm(dst, ones_rows[:, 0:T], bias_rows[:, 2 * P + 64 * h2:2 * P + 64 * h2 + 64],
                                      start=False, stop=True)
                    last.then_inc(S["v_ps"], 1)
                if has(b):
                    done(pe, "mlo", b)
                    for k in range(2):
                        for m in (mhi, mlo):
                            last = mm(ps_s[:, k, :], neg_id[:, :],
                                      m[:, p_b, 8 * k:8 * k + 8].unsqueeze(2).to_broadcast([P, 8, T]), start=False,
                                      stop=(m is mlo), skip_group_check=True)
                    last.then_inc(S["sm_ps"], 1)
                if has(d):
                    done(pe, "x3T", d)
                    mm(ps_d[0:HIDDEN, 2 * P:3 * P], w1_sb[:, :], x3T[:, p_d, :], start=True,
                       stop=True).then_inc(S["h_ps"], 1)
                if has(c):
                    done(pe, "att_b", c)
                    nc.tensor.transpose(ps_c[:, 0:P], att[:, :], id32[:, :]).then_inc(S["attT_ps"], 1)
                if has(a):
                    done(pe, "dup_k", a)
                    done(pe, "v_down", a)
                    for qk in range(2):
                        for g in range(QUADS):
                            at = P * (QUADS * qk + g)
                            src = parts[:, p_a, qk, 4 * g:4 * g + 4, :, :].rearrange("p h a d -> p (h a d)")
                            last = nc.tensor.transpose(ps_q[:, at:at + P], src, id16[:, :])
                    last.then_inc(S["qkT_ps"], 1)
                if has(d):
                    done(pe, "hT", d)
                    mm(ps_d[:, 384:384 + EXPERTS], hT[:, :], w2_sb[:, :], start=True, stop=True).then_inc(S["lg_ps"], 1)
                if has(c):
                    done(pe, "attT", c)
                    mm(ps_c[:, P:2 * P], attT[:, :], wfc[:, :], start=True, stop=False)
                    mm(ps_c[:, P:2 * P], ones_rows[:, :], bias_rows[:, 3 * P:4 * P], start=False, stop=True)
                    done(pe, "kv", c)
                    mm(ps_c[:, 2 * P:3 * P], decay_sb[:, :], kv[:, p_c, :], start=True, stop=True).then_inc(S["rs_ps"], 1)
                if has(d):
                    done(pe, "mask", d)
                    nc.tensor.transpose(ps_d[0:PARTS * EXPERTS, 448:512].bitcast(BF16),
                                        mask[:, p_d].rearrange("p c e -> p (c e)"), idb[:, :]).then_inc(S["maskT_ps"], 1)
                    if has(c):
                        done(pe, "eT_a", c)
                        done(pe, "eT_b", c)
                    for e in range(EXPERTS):
                        last = mm(ps_t[:, e // 4, P * (e % 4):P * (e % 4) + P],
                                  mask[:, p_d, 0, e:e + 1].to_broadcast([P, P]), idb[:, :], start=True, stop=True)
                    last.then_inc(S["mask_ps"], 1)
                if has(b):
                    done(pe, "exp", b)
                    done(pe, "xm", b - 2)
                    done(pe, "eT_b", b - 1)
                    for g in range(8):
                        last = nc.tensor.transpose(ps_t[:, g // 4, P * (g % 4):P * (g % 4) + P],
                                                   E[:, p_b, P * g:P * g + P], id32[:, :])
                    last.then_inc(S["eT_ps"], 1)
                if has(d):
                    done(pe, "xm", d)
                    done(pe, "maskT", d)
                    for e in range(EXPERTS):
                        mm(ps_d[:, 0:P], xm[:, e, :], ew_sb[:, e, :], start=(e == 0), stop=False)
                    mm(ps_d[:, 0:P], maskT[:, :], eb_rows[:, :], start=False, stop=True).then_inc(S["y_ps"], 1)

            pe.wait_ge(setup, SETUP)
            pe.wait_ge(rows_in, 16 * MOVES)
            steps(pe, step)


_INS = ["x", "ctx_1024", "L0_attn_w_qkv", "L0_attn_b_qkv", "L0_attn_w_fc", "L0_attn_b_fc", "L0_ffn_W1", "L0_ffn_b1",
        "L0_ffn_W2", "L0_ffn_b2", "L0_ffn_expert_W", "L0_ffn_expert_b"]


def tables():
    inv_freq = (1.0 / 10000.0 ** (np.arange(0, DEPTH, 2, dtype=np.float32) / DEPTH)).astype(np.float32)
    freqs = np.arange(HEADS, dtype=np.float32)[:, None] * inv_freq[None, :]
    rope = np.stack([np.tile(np.cos(freqs).reshape(-1), 2), np.tile(np.sin(freqs).reshape(-1), 2)]).astype(np.float32)
    t = np.arange(P)
    lag = t[None, :] - t[:, None]
    decay = np.where((lag >= 0) & (t[None, :] // T == t[:, None] // T), 0.9 ** np.maximum(lag, 0), 0.0)
    return {"rope": rope, "ident": np.eye(P, dtype=np.float32), "decay": decay.astype(np.float32),
            "first": np.arange(EXPERTS, 0, -1).astype(np.float32)}


def kernel(**inputs):
    import numpy as _np
    import concourse.bacc as _bacc
    from concourse import mybir as _mybir
    from concourse.bass_utils import run_bass_kernel_spmd as _run

    nc = _bacc.Bacc("TRN2", target_bir_lowering=False, num_devices=1)
    arrays, args = {}, []
    for name, a in [(n, inputs[n]) for n in _INS] + list(tables().items()):
        a = _np.ascontiguousarray(a)
        arrays[f"in_{name}_dram"] = a
        args.append(nc.dram_tensor(f"in_{name}_dram", a.shape, _mybir.dt.from_np(a.dtype), kind="ExternalInput").ap())
    shape = inputs["x"].shape
    args.append(nc.dram_tensor("out_0_dram", shape, _mybir.dt.float32, kind="ExternalOutput").ap())
    decoder_layer(nc, *args)
    r = _run(nc, [arrays], core_ids=[0])
    return r.results[0]["out_0_dram"]
```

```python
from contextlib import ExitStack

import numpy as np

import concourse.bass as bass
from concourse import mybir

ALU = mybir.AluOpType
ACT = mybir.ActivationFunctionType
F32 = mybir.dt.float32
F16 = mybir.dt.float16
BF16 = mybir.dt.bfloat16
AX_X = mybir.AxisListType.X

P = 128
T = 64
HEADS = 16
DEPTH = 8
QUADS = 4
PAIRS = 8
EXPERTS = 8
HIDDEN = 64
RING = 4
EPS = 1e-5
SCALE = float(DEPTH) ** -0.5
FCOL = DEPTH + 1
VCOL = 2 * 2 * FCOL
PARTS = 3


def decoder_layer(nc, x, ctx_in, w_qkv, b_qkv, w_fc, b_fc, w1, b1, w2, b2, ew, eb, rope, ident, decay, first, pick_part,
                  out):
    tiles = x.shape[0] * x.shape[1] // P
    x_t = x.rearrange("(n b) t d -> (b t) n d", b=2)
    ctx_t = ctx_in.rearrange("(n b) t d -> n (b t) d", b=2)
    out_t = out.rearrange("(n b) t d -> n (b t) d", b=2)

    with ExitStack() as stack:
        def sb(name, shape, dt=F32):
            return stack.enter_context(nc.sbuf_tensor(name, shape, dt))

        def sem(name):
            return stack.enter_context(nc.semaphore(name))

        w_all = sb("w_all", [P, 2, 3 * P])
        w_rot = sb("w_rot", [P, 2, 4 * P])
        rot = sb("rot", [P, 4, 2, P])
        rope_sb = sb("rope_sb", [P, 2, P])
        part_of = sb("part_of", [P, 2 * PARTS])
        res = sb("res", [PARTS, 2, 4 * P])
        bpart = sb("bpart", [PARTS, PARTS, 4 * P], BF16)
        brow = sb("brow", [PARTS, 2, 4 * P], BF16)
        bias_rows = sb("bias_rows", [PARTS, 4 * P], BF16)
        ones_rows = sb("ones_rows", [PARTS, P], BF16)
        wfc = sb("wfc", [P, P])
        w1_sb = sb("w1_sb", [P, HIDDEN])
        b1_sb = sb("b1_sb", [HIDDEN, 1])
        w2_sb = sb("w2_sb", [HIDDEN, EXPERTS])
        b2_sb = sb("b2_sb", [P, EXPERTS])
        first_sb = sb("first_sb", [P, EXPERTS])
        ew_sb = sb("ew_sb", [P, EXPERTS, P])
        eb_sb = sb("eb_sb", [PARTS * EXPERTS, P])
        eres = sb("eres", [PARTS * EXPERTS, 2, P])
        epart = sb("epart", [PARTS * EXPERTS, PARTS, P], BF16)
        erow = sb("erow", [PARTS * EXPERTS, 4, P], BF16)
        eb_rows = sb("eb_rows", [PARTS * EXPERTS, P], BF16)
        id32 = sb("id32", [P, P])
        id16 = sb("id16", [P, P], F16)
        idb = sb("idb", [P, P], BF16)
        neg_id = sb("neg_id", [P, P], BF16)
        decay_sb = sb("decay_sb", [P, P])
        eps_sb = sb("eps_sb", [P, 1])
        half = sb("half", [P, 1])
        zero = sb("zero", [P, 1])

        X = sb("X", [P, tiles, P])
        C = sb("C", [P, RING, P])
        st = sb("st", [P, 3, 2, 6])
        mv = sb("mv", [P, 3, 2, 2])
        ve = sb("ve", [P, 3, 1])
        rstd = sb("rstd", [P, 3, 2, 1])
        mr = sb("mr", [P, 3, 1])
        nmr = sb("nmr", [P, 3, 2, 1])
        xn1 = sb("xn1", [P, 2, P])
        xT = sb("xT", [P, 2, P])
        parts = sb("parts", [P, 2, 2, HEADS, 4, DEPTH], F16)
        qkT = sb("qkT", [P, 2, 2, QUADS, P], F16)
        V = sb("V", [P, RING, 2, PAIRS * VCOL], F16)
        mx = sb("mx", [P, 2, HEADS])
        mhi = sb("mhi", [P, 2, HEADS], BF16)
        mlo = sb("mlo", [P, 2, HEADS], BF16)
        E = sb("E", [P, 2, 2 * 512])
        ET = sb("ET", [P, 2, 2, PAIRS, P], F16)
        rec = sb("rec", [P, HEADS])
        att = sb("att", [P, P])
        attT = sb("attT", [P, P])
        x1 = sb("x1", [P, 2, P])
        kv = sb("kv", [P, 2, P])
        gated = sb("gated", [P, P])
        x2 = sb("x2", [P, RING, P])
        xn3 = sb("xn3", [P, 2, P])
        x3T = sb("x3T", [P, 2, P])
        hT = sb("hT", [HIDDEN, P])
        lg = sb("lg", [P, EXPERTS])
        top = sb("top", [P, 2])
        pick = sb("pick", [P, EXPERTS])
        mask = sb("mask", [P, 2, PARTS, EXPERTS], BF16)
        maskT = sb("maskT", [PARTS * EXPERTS, P], BF16)
        late = sb("late", [P, 4 * P], BF16)
        xm = sb("xm", [P, EXPERTS, P])
        O = sb("O", [P, RING, P])

        ps_s = stack.enter_context(nc.psum_tensor("ps_s", [P, 2, 512], F32))
        ps_t = stack.enter_context(nc.psum_tensor("ps_t", [P, 2, 512], F32))
        ps_p = stack.enter_context(nc.psum_tensor("ps_p", [P, 512], F32))
        ps_q = stack.enter_context(nc.psum_tensor("ps_q", [P, 1024], F16))
        ps_c = stack.enter_context(nc.psum_tensor("ps_c", [P, 512], F32))
        ps_d = stack.enter_context(nc.psum_tensor("ps_d", [P, 512], F32))
        ps_v = ps_q[:, 0:2 * P].bitcast(F32)

        x_in = sem("x_in")
        c_in = [sem(f"c_in{u}") for u in range(RING)]
        o_out = [sem(f"o_out{u}") for u in range(RING)]
        w_ident, w_in_qkv, w_in_b, w_in_rest, w_in_eb = (sem(n) for n in (
            "w_ident", "w_in_qkv", "w_in_b", "w_in_rest", "w_in_eb"))
        made = sem("made")
        v_zero = sem("v_zero")
        eb_made = sem("eb_made")
        id_made = sem("id_made")
        names = ("st1 mv1 ve1 rstd1 mr1 nmr1 xn1 xT_ps xT s_0 s_2 s_1 qk_ps v_ps hi lo_q lo_k dup_q dup_k v_up v_down "
                 "vl_up vl_down qkT_ps qkT s_ps mx mhi mlo sm_ps exp eT_ps eT_a eT_b el_a el_b pv_ps rec_a rec_b att_a "
                 "att_b attT_ps attT kv rs_ps x1 st2 mv2 ve2 rstd2 gated x2 st3 mv3 ve3 rstd3 mr3 nmr3 xn3 x3T_ps x3T "
                 "h_ps hT lg_ps lg top1 pick top2 mask maskT_ps maskT mask_ps late xm xm_late y_ps o").split()
        S = {n: sem("s_" + n) for n in names}

        def done(eng, name, t):
            if isinstance(t, int) and t < 0:
                return
            eng.wait_ge(S[name], t + 1)

        def has(t):
            return not isinstance(t, int) or 0 <= t < tiles

        def steps(eng, step):
            begin, end = 2 * RING, (tiles - 1) // RING * RING
            for s in range(-1, begin):
                step(s, s % RING)
            with eng.Fori(begin, end, RING) as s0:
                for u in range(RING):
                    step(s0 + u, u)
            for s in range(end, tiles + 7):
                step(s, s % RING)

        def ring_count(t, slot):
            if isinstance(t, int):
                return 16 * (t // RING + 1)
            return (t - slot) * (16 // RING) + 16

        def x_of(t):
            return X[:, bass.ds(t, 1), :].rearrange("p a d -> p (a d)")

        def row(ap):
            return ap.rearrange("(a n) -> a n", a=1)

        def v_views(h2, slot):
            rows = slice(T * h2, T * h2 + T)
            src = ps_v[rows, :].rearrange("p (b g d) -> p b g d", b=2, d=DEPTH)
            return src, [V[rows, slot, part, :].rearrange("p (g b h f) -> p h b g f", b=2, h=2, f=FCOL)[
                :, h2, :, :, 0:DEPTH] for part in range(2)]

        V_ZERO = 1 + 2 * RING + 4
        EB_MADE = 10
        MADE_QKV = 4 + 4 + 2
        MADE = MADE_QKV + 8

        block = stack.enter_context(nc.Block())

        @block.sync
        def _(sp):
            def step(s, u):
                n, o = s + 1, s - 7
                if has(n) and not (isinstance(n, int) and n < RING):
                    done(sp, "kv", n - RING)
                    sp.dma_start(C[:, (u + 1) % RING, :], ctx_t[bass.ds(n, 1)].rearrange("a p d -> p (a d)")).then_inc(
                        c_in[(u + 1) % RING], 16)
                if has(o):
                    done(sp, "o", o)
                    sp.dma_start(out_t[bass.ds(o, 1)].rearrange("a p d -> p (a d)"), O[:, (u - 7) % RING, :]).then_inc(
                        o_out[(u - 7) % RING], 16)

            sp.dma_start(X[:, 0:RING, :], x_t[:, 0:RING, :]).then_inc(x_in, 16)
            sp.dma_start(part_of[:, :], pick_part).then_inc(w_in_b, 16)
            sp.dma_start(w_rot[:, 1, 3 * P:], row(b_fc).to_broadcast([P, P])).then_inc(w_in_b, 16)
            fc_rows = w_fc.rearrange("(g j d) n -> j g d n", j=4, d=DEPTH)
            for j in range(4):
                sp.dma_start(wfc[32 * j:32 * j + 32, :], fc_rows[j]).then_inc(w_in_rest, 16)
            sp.dma_start(decay_sb[:, :], decay).then_inc(w_in_rest, 16)
            for t in range(RING):
                sp.dma_start(C[:, t, :], ctx_t[t]).then_inc(c_in[t], 16)
            for n in range(1, tiles // RING):
                sp.wait_ge(x_in, 16 * n)
                sp.dma_start(X[:, RING * n:RING * n + RING, :], x_t[:, RING * n:RING * n + RING, :]).then_inc(x_in, 16)
            steps(sp, step)
            for u in range(RING):
                sp.wait_ge(o_out[u], 16 * (tiles // RING))

        @block.gpsimd
        def _(pool):
            g = nc.gpsimd
            count = 0

            def link(ins, counter):
                nonlocal count
                count += 1
                ins.then_inc(counter, 1)
                pool.wait_ge(counter, count)

            g.memset(eps_sb[:, :], EPS).then_inc(v_zero, 1)
            g.memset(half[:, :], -0.5).then_inc(v_zero, 1)
            g.memset(zero[:, :], 0.0).then_inc(v_zero, 1)
            g.memset(ones_rows[:, :], 1.0).then_inc(v_zero, 1)
            count = 4
            link(g.memset(V[:, :, :, :].rearrange("p r c n -> p (r c n)").bitcast(F32), 0.0), v_zero)
            for h2 in range(2):
                for r in range(RING):
                    ones = V[T * h2:T * h2 + T, r, 0, :].rearrange("p (g b h f) -> p g b h f", b=2, h=2, f=FCOL)
                    g.memset(ones[:, :, :, h2, DEPTH], 1.0).then_inc(v_zero, 1)

            def root(n, t, p):
                done(pool, f"mv{n}", t)
                g.tensor_tensor(ve[:, n - 1, :], mv[:, n - 1, p, 1:2], eps_sb[:, :], ALU.add).then_inc(S[f"ve{n}"], 1)
                done(pool, f"ve{n}", t)
                g.tensor_tensor(rstd[:, n - 1, p, :], ve[:, n - 1, :], half[:, :], ALU.pow).then_inc(S[f"rstd{n}"], 1)
                if n != 2:
                    done(pool, f"rstd{n}", t)
                    g.tensor_tensor(mr[:, n - 1, :], mv[:, n - 1, p, 0:1], rstd[:, n - 1, p, :],
                                    ALU.mult).then_inc(S[f"mr{n}"], 1)
                    done(pool, f"mr{n}", t)
                    g.tensor_tensor(nmr[:, n - 1, p, :], zero[:, :], mr[:, n - 1, :],
                                    ALU.subtract).then_inc(S[f"nmr{n}"], 1)

            def step(s, u):
                z, c, n, e = s + 1, s - 3, s - 4, s - 6
                odd, even = (u + 1) % 2, u % 2
                if has(n):
                    root(3, n, even)
                if has(z):
                    root(1, z, odd)
                if has(c):
                    pool.wait_ge(c_in[(u - 3) % RING], ring_count(c, (u - 3) % RING))
                    done(pool, "rs_ps", c - 2)
                    cc = C[:, (u - 3) % RING, :]
                    g.tensor_tensor(kv[:, odd, :], cc, cc, ALU.mult).then_inc(S["kv"], 1)
                if has(e):
                    done(pool, "late", e)
                    done(pool, "y_ps", e - 1)
                    g.tensor_tensor(xm[:, 4:, :], x3T[:, even, :].unsqueeze(1).to_broadcast([P, 4, P]),
                                    late[:, :].rearrange("p (e t) -> p e t", t=P), ALU.mult).then_inc(S["xm_late"], 1)
                if has(c):
                    root(2, c, odd)

            count = 0
            pool.wait_ge(w_in_eb, 16 * PARTS)
            pool.wait_ge(w_in_b, 32)
            n24 = PARTS * EXPERTS
            link(g.tensor_copy(epart[:, 0, :], eb_sb[:, :]), eb_made)
            link(g.tensor_tensor(eres[:, 0, :], eb_sb[:, :], epart[:, 0, :], ALU.subtract), eb_made)
            link(g.tensor_copy(epart[:, 1, :], eres[:, 0, :]), eb_made)
            link(g.tensor_tensor(eres[:, 1, :], eres[:, 0, :], epart[:, 1, :], ALU.subtract), eb_made)
            link(g.tensor_copy(epart[:, 2, :], eres[:, 1, :]), eb_made)
            for c in range(PARTS):
                link(g.tensor_scalar(erow[:, c, :], epart[:, c, :], part_of[0:n24, PARTS + c:PARTS + c + 1], None,
                                     ALU.mult), eb_made)
            link(g.tensor_tensor(erow[:, 3, :], erow[:, 0, :], erow[:, 1, :], ALU.add), eb_made)
            link(g.tensor_tensor(eb_rows[:, :], erow[:, 3, :], erow[:, 2, :], ALU.add), eb_made)
            assert count == EB_MADE
            steps(pool, step)

        @block.vector
        def _(dve):
            v = nc.vector
            count = 0

            def link(ins):
                nonlocal count
                count += 1
                ins.then_inc(made, 1)
                dve.wait_ge(made, count)

            def setup_qkv():
                nonlocal count
                dve.wait_ge(w_in_qkv, 48)
                src = w_all[:, :, 0:2 * P].rearrange("p b (m e) -> p b e m", e=2)
                dst = w_rot[:, :, 0:2 * P].rearrange("p b (m e) -> p b e m", e=2)
                for q, (e, cs) in enumerate(((0, 0), (1, 1), (0, 1), (1, 0))):
                    v.tensor_tensor(rot[:, q, :, :], src[:, :, e, :],
                                    rope_sb[:, cs, :].unsqueeze(1).to_broadcast([P, 2, P]), ALU.mult).then_inc(made, 1)
                for b in range(2):
                    for h2 in range(2):
                        s_ = w_all[:, b, 2 * P:].rearrange("p (g h j d) -> p h j g d", g=2, h=2, j=4)[:, h2]
                        d_ = w_rot[:, b, 2 * P:3 * P].rearrange("p (h j g d) -> p h j g d", g=2, h=2, j=4)[:, h2]
                        if b + h2 < 2:
                            v.tensor_copy(d_, s_).then_inc(made, 1)
                        else:
                            count = 7
                            link(v.tensor_copy(d_, s_))
                v.tensor_tensor(dst[:, :, 0, :], rot[:, 0], rot[:, 1], ALU.subtract).then_inc(made, 1)
                count = 9
                link(v.tensor_tensor(dst[:, :, 1, :], rot[:, 2], rot[:, 3], ALU.add))

            def setup_bias():
                dve.wait_ge(w_in_b, 32)
                whole = w_rot[0:PARTS, 1, :]
                link(v.tensor_copy(bpart[:, 0, :], whole))
                link(v.tensor_tensor(res[:, 0, :], whole, bpart[:, 0, :], ALU.subtract))
                link(v.tensor_copy(bpart[:, 1, :], res[:, 0, :]))
                link(v.tensor_tensor(res[:, 1, :], res[:, 0, :], bpart[:, 1, :], ALU.subtract))
                link(v.tensor_copy(bpart[:, 2, :], res[:, 1, :]))
                link(v.tensor_scalar(brow[:, 0, :], bpart[:, 0, :], part_of[0:PARTS, 0:1], None, ALU.mult))
                for c, dst in ((1, brow[:, 1, :]), (2, bias_rows[:, :])):
                    link(v.scalar_tensor_tensor(out=dst, in0=bpart[:, c, :], scalar=part_of[0:PARTS, c:c + 1],
                                                in1=brow[:, c - 1, :], op0=ALU.mult, op1=ALU.add))
                assert count == MADE, count

            def step(s, u):
                z, a, b, p, c, r, e, o = s + 1, s, s - 1, s - 2, s - 3, s - 5, s - 6, s - 7
                odd, even = (u + 1) % 2, u % 2

                if has(o):
                    slot = (u - 7) % RING
                    done(dve, "y_ps", o)
                    if not (isinstance(o, int) and o < RING):
                        dve.wait_ge(o_out[slot], ring_count(o - RING, slot))
                    v.tensor_tensor(O[:, slot, :], ps_d[:, 0:P], x2[:, slot, :], ALU.add).then_inc(S["o"], 1)
                if has(z):
                    group = z // RING if isinstance(z, int) else None
                    dve.wait_ge(x_in, 16 * (group + 1) if group is not None else ring_count(z, (u + 1) % RING))
                    dve.nop(nofuse=True)
                    v.bn_stats(st[:, 0, odd, :], x_of(z)).then_inc(S["st1"], 1)
                if has(p):
                    done(dve, "pv_ps", p - 2)
                    for k, (hi, lo) in enumerate((("eT_a", "el_a"), ("eT_b", "el_b"))):
                        done(dve, hi, p)
                        if has(z) and k == 0:
                            done(dve, "st1", z)
                        v.tensor_tensor(ET[:, even, 1, 4 * k:4 * k + 4, :].rearrange("p g t -> p (g t)"), ps_t[:, k, :],
                                        ET[:, even, 0, 4 * k:4 * k + 4, :].rearrange("p g t -> p (g t)"),
                                        ALU.subtract).then_inc(S[lo], 1)
                        if has(z) and k == 0:
                            v.bn_aggr(mv[:, 0, odd, :], st[:, 0, odd, :]).then_inc(S["mv1"], 1)
                elif has(z):
                    done(dve, "st1", z)
                    v.bn_aggr(mv[:, 0, odd, :], st[:, 0, odd, :]).then_inc(S["mv1"], 1)
                if has(b):
                    done(dve, "s_ps", b)
                    v.tensor_reduce(mx[:, odd, :], ps_s[:, :, :].rearrange("p k (h t) -> p (k h) t", t=T), AX_X,
                                    ALU.max).then_inc(S["mx"], 1)
                    done(dve, "mx", b)
                    v.tensor_copy(mhi[:, odd, :], mx[:, odd, :]).then_inc(S["mhi"], 1)
                    done(dve, "mhi", b)
                    v.tensor_tensor(mlo[:, odd, :], mx[:, odd, :], mhi[:, odd, :], ALU.subtract).then_inc(S["mlo"], 1)
                if has(a):
                    done(dve, "qk_ps", a)
                    done(dve, "hi", a)
                    for qk, lo in enumerate(("lo_q", "lo_k")):
                        mine = parts[:, even, qk]
                        v.tensor_tensor(mine[:, :, 2 - qk, :],
                                        ps_p[:, P * qk:P * qk + P].rearrange("p (h d) -> p h d", d=DEPTH),
                                        mine[:, :, 0, :], ALU.subtract).then_inc(S[lo], 1)
                    done(dve, "lo_q", a)
                    pairs = parts[:, even, 0].rearrange("p h (a c) d -> p h c a d", c=2)
                    v.tensor_copy(pairs[:, :, 1], pairs[:, :, 0]).then_inc(S["dup_q"], 1)
                    done(dve, "lo_k", a)
                    v.tensor_copy(parts[:, even, 1, :, 2:4, :], parts[:, even, 1, :, 0:2, :]).then_inc(S["dup_k"], 1)
                    done(dve, "v_up", a)
                    done(dve, "v_down", a)
                    for h2, name in ((0, "vl_up"), (1, "vl_down")):
                        src, (v_hi, v_lo) = v_views(h2, u)
                        v.tensor_tensor(v_lo, src, v_hi, ALU.subtract).then_inc(S[name], 1)
                if has(e):
                    done(dve, "mask_ps", e)
                    done(dve, "x3T", e)
                    done(dve, "y_ps", e - 1)
                    v.tensor_tensor(xm[:, 0:4, :], x3T[:, even, :].unsqueeze(1).to_broadcast([P, 4, P]),
                                    ps_t[:, 0, :].rearrange("p (e t) -> p e t", t=P), ALU.mult).then_inc(S["xm"], 1)
                if has(c):
                    done(dve, "rs_ps", c)
                    v.tensor_tensor(x1[:, odd, :], ps_c[:, P:2 * P], x_of(c), ALU.add).then_inc(S["x1"], 1)
                if has(r):
                    done(dve, "lg_ps", r)
                    v.tensor_tensor(lg[:, :], ps_d[:, 384:384 + EXPERTS], b2_sb[:, :], ALU.add).then_inc(S["lg"], 1)
                if has(c):
                    done(dve, "x1", c)
                    v.bn_stats(st[:, 1, odd, :], x1[:, odd, :]).then_inc(S["st2"], 1)
                if has(r):
                    done(dve, "lg", r)
                    if has(c):
                        done(dve, "st2", c)
                    v.tensor_reduce(top[:, 0:1], lg[:, :], AX_X, ALU.max).then_inc(S["top1"], 1)
                if has(c):
                    if isinstance(s, int):
                        done(dve, "st2", c)
                    v.bn_aggr(mv[:, 1, odd, :], st[:, 1, odd, :]).then_inc(S["mv2"], 1)
                if has(c):
                    done(dve, "mv2", c)
                    done(dve, "o", c - RING)
                    v.scalar_tensor_tensor(out=gated[:, :], in0=x1[:, odd, :], scalar=mv[:, 1, odd, 0:1],
                                           in1=ps_c[:, 2 * P:3 * P], op0=ALU.subtract,
                                           op1=ALU.mult).then_inc(S["gated"], 1)
                if has(r):
                    done(dve, "top1", r)
                    v.scalar_tensor_tensor(out=pick[:, :], in0=lg[:, :], scalar=top[:, 0:1], in1=first_sb[:, :],
                                           op0=ALU.is_ge, op1=ALU.mult).then_inc(S["pick"], 1)
                if has(p):
                    done(dve, "pv_ps", p)
                    done(dve, "attT_ps", p - 1)
                    halves = []
                    for b_ in range(2):
                        lo, hi = T * b_, T * b_ + T
                        got = ps_p[lo:hi, 0:PAIRS * VCOL].rearrange("p (g b h f) -> p b g h f", b=2, h=2, f=FCOL)[:, b_]
                        over = rec[lo:hi, :].rearrange("p (g h) -> p g h", h=2)
                        v.reciprocal(over, got[:, :, :, DEPTH]).then_inc(S["rec_a" if b_ == 0 else "rec_b"], 1)
                        halves.append((lo, hi, got, over))
                if has(p):
                    for b_, (lo, hi, got, over) in enumerate(halves):
                        done(dve, "rec_a" if b_ == 0 else "rec_b", p)
                        v.tensor_tensor(att[lo:hi, :].rearrange("p (g h f) -> p g h f", h=2, f=DEPTH),
                                        got[:, :, :, 0:DEPTH], over.unsqueeze(3).to_broadcast([T, PAIRS, 2, DEPTH]),
                                        ALU.mult).then_inc(S["att_a" if b_ == 0 else "att_b"], 1)
                if has(c):
                    done(dve, "gated", c)
                    done(dve, "rstd2", c)
                    v.scalar_tensor_tensor(out=x2[:, (u - 3) % RING, :], in0=gated[:, :], scalar=rstd[:, 1, odd, :],
                                           in1=x1[:, odd, :], op0=ALU.mult, op1=ALU.add).then_inc(S["x2"], 1)
                if has(r):
                    done(dve, "pick", r)
                    v.tensor_reduce(top[:, 1:2], pick[:, :], AX_X, ALU.max).then_inc(S["top2"], 1)
                if has(c):
                    done(dve, "x2", c)
                    v.bn_stats(st[:, 2, odd, :], x2[:, (u - 3) % RING, :]).then_inc(S["st3"], 1)
                if has(r):
                    done(dve, "top2", r)
                    if has(c):
                        done(dve, "st3", c)
                    v.tensor_scalar(mask[:, odd, :, :], pick[:, :].unsqueeze(1).to_broadcast([P, PARTS, EXPERTS]),
                                    top[:, 1:2], None, ALU.is_equal).then_inc(S["mask"], 1)
                if has(c):
                    if isinstance(s, int):
                        done(dve, "st3", c)
                    v.bn_aggr(mv[:, 2, odd, :], st[:, 2, odd, :]).then_inc(S["mv3"], 1)

            setup_qkv()
            setup_bias()
            steps(dve, step)

        @block.scalar
        def _(act):
            sc = nc.scalar
            act.dma_start(id32[:, :], ident).then_inc(w_ident, 16)
            act.dma_start(w_all[:, 0, :], w_qkv).then_inc(w_in_qkv, 16)
            act.dma_start(w_all[:, 1, :], row(b_qkv).to_broadcast([P, 3 * P])).then_inc(w_in_qkv, 16)
            act.dma_start(rope_sb[:, :, :], rope.rearrange("(a c) n -> a c n", a=1).to_broadcast([P, 2, P])).then_inc(
                w_in_qkv, 16)
            act.wait_ge(w_ident, 16)
            sc.copy(id16[:, :], id32[:, :]).then_inc(id_made, 1)
            sc.copy(idb[:, :], id32[:, :]).then_inc(id_made, 1)
            sc.mul(neg_id[:, :], id32[:, :], -1.0).then_inc(id_made, 1)
            for dst, src in ((w1_sb[:, :], w1), (b1_sb[:, :], b1.rearrange("(n a) -> n a", a=1)), (w2_sb[:, :], w2),
                             (b2_sb[:, :], row(b2).to_broadcast([P, EXPERTS])),
                             (first_sb[:, :], row(first).to_broadcast([P, EXPERTS])),
                             (ew_sb[:, :, :], ew.rearrange("e k n -> k e n"))):
                act.dma_start(dst, src).then_inc(w_in_rest, 16)
            for c in range(PARTS):
                act.dma_start(eb_sb[EXPERTS * c:EXPERTS * c + EXPERTS, :], eb).then_inc(w_in_eb, 16)

            def step(s, u):
                z, a, b, p, c, n, r, e = s + 1, s, s - 1, s - 2, s - 3, s - 4, s - 5, s - 6
                odd, even = (u + 1) % 2, u % 2
                if has(p):
                    done(act, "eT_ps", p)
                    done(act, "pv_ps", p - 2)
                    for k, name in enumerate(("eT_a", "eT_b")):
                        sc.copy(ET[:, even, 0, 4 * k:4 * k + 4, :].rearrange("p g t -> p (g t)"),
                                ps_t[:, k, :]).then_inc(S[name], 1)
                if has(a):
                    done(act, "xT_ps", a)
                    done(act, "v_ps", a - 2)
                    sc.copy(xT[:, even, :], ps_p[:, 0:P]).then_inc(S["xT"], 1)
                if has(e):
                    done(act, "maskT_ps", e)
                    done(act, "y_ps", e - 1)
                    if has(r):
                        done(act, "x3T_ps", r)
                    sc.copy(maskT[:, :], ps_d[0:PARTS * EXPERTS, 448:512].bitcast(BF16)).then_inc(S["maskT"], 1)
                if has(r):
                    done(act, "x3T_ps", r)
                    done(act, "xm", r - 2)
                    done(act, "xm_late", r - 2)
                    sc.copy(x3T[:, odd, :], ps_d[:, P:2 * P]).then_inc(S["x3T"], 1)
                if has(c):
                    done(act, "attT_ps", c)
                    done(act, "rs_ps", c - 1)
                    sc.copy(attT[:, :], ps_c[:, 0:P]).then_inc(S["attT"], 1)
                if has(a):
                    done(act, "qk_ps", a)
                    done(act, "qkT_ps", a - 2)
                    sc.copy(parts[:, even, :, :, 0, :].rearrange("p q h d -> p (q h) d"),
                            ps_p[:, 0:2 * P].rearrange("p (h d) -> p h d", d=DEPTH)).then_inc(S["hi"], 1)
                if has(r):
                    done(act, "h_ps", r)
                    done(act, "lg_ps", r - 1)
                    sc.activation(hT[:, :], ps_d[0:HIDDEN, 2 * P:3 * P], ACT.Relu, bias=b1_sb[:, :]).then_inc(S["hT"], 1)
                if has(a):
                    done(act, "v_ps", a)
                    done(act, "pv_ps", a - RING)
                    for h2, name in ((0, "v_up"), (1, "v_down")):
                        src, (v_hi, _) = v_views(h2, u)
                        sc.copy(v_hi, src).then_inc(S[name], 1)
                if has(e):
                    done(act, "mask_ps", e)
                    done(act, "xm_late", e - 1)
                    sc.copy(late[:, :], ps_t[:, 1, :]).then_inc(S["late"], 1)
                if has(n):
                    done(act, "nmr3", n)
                    done(act, "x3T_ps", n - 2)
                    act.nop(nofuse=True)
                    sc.activation(xn3[:, even, :], x2[:, (u - 4) % RING, :], ACT.Identity, scale=rstd[:, 2, even, :],
                                  bias=nmr[:, 2, even, :]).then_inc(S["xn3"], 1)
                if has(z):
                    done(act, "nmr1", z)
                    done(act, "xT_ps", z - 2)
                    act.nop(nofuse=True)
                    sc.activation(xn1[:, odd, :], x_of(z), ACT.Identity, scale=rstd[:, 0, odd, :],
                                  bias=nmr[:, 0, odd, :]).then_inc(S["xn1"], 1)
                if has(b):
                    done(act, "sm_ps", b)
                    done(act, "eT_ps", b - 2)
                    sc.activation(E[:, odd, :], ps_s[:, :, :].rearrange("p k n -> p (k n)"), ACT.Exp,
                                  scale=SCALE).then_inc(S["exp"], 1)
                if has(a):
                    done(act, "qkT_ps", a)
                    done(act, "s_ps", a - 2)
                    sc.copy(qkT[:, even, :, :, :].rearrange("p q g t -> p (q g t)"), ps_q[:, :]).then_inc(S["qkT"], 1)

            steps(act, step)

        @block.tensor
        def _(pe):
            mm = nc.tensor.matmul

            def step(s, u):
                a, b, p, c, r, e = s, s - 1, s - 2, s - 3, s - 5, s - 6
                odd, even = (u + 1) % 2, u % 2
                if has(p):
                    done(pe, "exp", p)
                    done(pe, "xm", p - 5)
                    done(pe, "late", p - 5)
                    for g in range(PAIRS):
                        last = nc.tensor.transpose(ps_t[:, g // 4, P * (g % 4):P * (g % 4) + P],
                                                   E[:, even, P * g:P * g + P], id32[:, :])
                    last.then_inc(S["eT_ps"], 1)
                if has(a):
                    done(pe, "xn1", a)
                    done(pe, "att_b", a - 3)
                    done(pe, "lo_k", a - 1)
                    nc.tensor.transpose(ps_p[:, 0:P], xn1[:, even, :], id32[:, :]).then_inc(S["xT_ps"], 1)
                if has(e):
                    done(pe, "mask", e)
                    done(pe, "o", e - 1)
                    nc.tensor.transpose(ps_d[0:PARTS * EXPERTS, 448:512].bitcast(BF16),
                                        mask[:, even].rearrange("p c e -> p (c e)"), idb[:, :]).then_inc(S["maskT_ps"], 1)
                if has(r):
                    done(pe, "xn3", r)
                    done(pe, "lg", r - 1)
                    done(pe, "o", r - 2)
                    nc.tensor.transpose(ps_d[:, P:2 * P], xn3[:, odd, :], id32[:, :]).then_inc(S["x3T_ps"], 1)
                if has(c):
                    done(pe, "att_b", c)
                    done(pe, "gated", c - 1)
                    nc.tensor.transpose(ps_c[:, 0:P], att[:, :], id32[:, :]).then_inc(S["attT_ps"], 1)
                if has(b):
                    done(pe, "qkT", b)
                    done(pe, "exp", b - 1)
                    for j in (0, 2, 1, 3):
                        rows = slice(32 * j, 32 * j + 32)
                        if j % 2:
                            done(pe, f"s_{j - 1}", b)
                        for g in range(QUADS):
                            for b_ in range(2):
                                t = slice(T * b_, T * b_ + T)
                                at = 256 * (j % 2) + 64 * g
                                last = mm(ps_s[t, j // 2, at:at + T], qkT[rows, odd, 0, g, t], qkT[rows, odd, 1, g, t],
                                          start=(j in (0, 2) and g == 0), stop=False, skip_group_check=True)
                        if j < 3:
                            last.then_inc(S[f"s_{j}"], 1)
                    last.then_inc(S["s_ps"], 1)
                if has(a):
                    if isinstance(a, int) and a == 0:
                        pe.wait_ge(v_zero, V_ZERO)
                        pe.wait_ge(made, MADE)
                    done(pe, "xT", a)
                    mm(ps_p[:, 0:2 * P], xT[:, even, :], w_rot[:, 0, 0:2 * P], start=True, stop=False)
                    mm(ps_p[:, 0:2 * P], ones_rows[:, :], bias_rows[:, 0:2 * P], start=False,
                       stop=True).then_inc(S["qk_ps"], 1)
                if has(r):
                    done(pe, "x3T", r)
                    if has(e):
                        done(pe, "maskT", e)
                    mm(ps_d[0:HIDDEN, 2 * P:3 * P], w1_sb[:, :], x3T[:, odd, :], start=True,
                       stop=True).then_inc(S["h_ps"], 1)
                if has(a):
                    done(pe, "qkT", a - 1)
                    for b_ in range(2):
                        for h2 in range(2):
                            dst = ps_v[T * h2:T * h2 + T, T * b_:T * b_ + T]
                            cols = slice(2 * P + T * h2, 2 * P + T * h2 + T)
                            mm(dst, xT[:, even, T * b_:T * b_ + T], w_rot[:, 0, cols], start=True, stop=False)
                            last = mm(dst, ones_rows[:, 0:T], bias_rows[:, cols], start=False, stop=True)
                    last.then_inc(S["v_ps"], 1)
                if has(e):
                    done(pe, "mask", e)
                    if has(p):
                        done(pe, "el_b", p)
                    for x_ in range(EXPERTS):
                        last = mm(ps_t[:, x_ // 4, P * (x_ % 4):P * (x_ % 4) + P],
                                  mask[:, even, 0, x_:x_ + 1].to_broadcast([P, P]), idb[:, :], start=True, stop=True)
                    last.then_inc(S["mask_ps"], 1)
                if has(c):
                    if isinstance(c, int) and c == 0:
                        pe.wait_ge(w_in_rest, 16 * 11)
                    done(pe, "attT", c)
                    mm(ps_c[:, P:2 * P], attT[:, :], wfc[:, :], start=True, stop=False)
                    mm(ps_c[:, P:2 * P], ones_rows[:, :], bias_rows[:, 3 * P:4 * P], start=False, stop=True)
                    done(pe, "kv", c)
                    mm(ps_c[:, 2 * P:3 * P], decay_sb[:, :], kv[:, odd, :], start=True, stop=True).then_inc(S["rs_ps"], 1)
                if has(r):
                    done(pe, "hT", r)
                    mm(ps_d[:, 384:384 + EXPERTS], hT[:, :], w2_sb[:, :], start=True, stop=True).then_inc(S["lg_ps"], 1)
                if has(b):
                    done(pe, "mlo", b)
                    for k in range(2):
                        for m in (mhi, mlo):
                            last = mm(ps_s[:, k, :], neg_id[:, :],
                                      m[:, odd, 8 * k:8 * k + 8].unsqueeze(2).to_broadcast([P, 8, T]), start=False,
                                      stop=(m is mlo), skip_group_check=True)
                    last.then_inc(S["sm_ps"], 1)
                if has(a):
                    done(pe, "dup_k", a)
                    done(pe, "vl_down", a)
                    for qk in range(2):
                        for g in range(QUADS):
                            at = P * (QUADS * qk + g)
                            src = parts[:, even, qk, 4 * g:4 * g + 4, :, :].rearrange("p h a d -> p (h a d)")
                            last = nc.tensor.transpose(ps_q[:, at:at + P], src, id16[:, :])
                    last.then_inc(S["qkT_ps"], 1)
                if has(p):
                    done(pe, "el_b", p)
                    if has(a):
                        done(pe, "lo_k", a)
                    slot = (u - 2) % RING
                    for g in range(PAIRS):
                        cols = slice(VCOL * g, VCOL * g + VCOL)
                        mm(ps_p[:, cols], ET[:, even, 0, g, :], V[:, slot, 0, cols], start=True, stop=False)
                        mm(ps_p[:, cols], ET[:, even, 0, g, :], V[:, slot, 1, cols], start=False, stop=False)
                        last = mm(ps_p[:, cols], ET[:, even, 1, g, :], V[:, slot, 0, cols], start=False, stop=True)
                    last.then_inc(S["pv_ps"], 1)

                if has(e):
                    done(pe, "xm", e)
                    done(pe, "xm_late", e)
                    if isinstance(e, int) and e == 0:
                        pe.wait_ge(eb_made, EB_MADE)
                    if has(r):
                        done(pe, "lg", r)
                    done(pe, "maskT", e)
                    for x_ in range(EXPERTS):
                        mm(ps_d[:, 0:P], xm[:, x_, :], ew_sb[:, x_, :], start=(x_ == 0), stop=False)
                    mm(ps_d[:, 0:P], maskT[:, :], eb_rows[:, :], start=False, stop=True).then_inc(S["y_ps"], 1)

            pe.wait_ge(w_ident, 16)
            pe.wait_ge(id_made, 3)
            steps(pe, step)


_INS = ["x", "ctx_1024", "L0_attn_w_qkv", "L0_attn_b_qkv", "L0_attn_w_fc", "L0_attn_b_fc", "L0_ffn_W1", "L0_ffn_b1",
        "L0_ffn_W2", "L0_ffn_b2", "L0_ffn_expert_W", "L0_ffn_expert_b"]


def tables():
    inv_freq = (1.0 / 10000.0 ** (np.arange(0, DEPTH, 2, dtype=np.float32) / DEPTH)).astype(np.float32)
    freqs = np.arange(HEADS, dtype=np.float32)[:, None] * inv_freq[None, :]
    rope = np.stack([np.tile(np.cos(freqs).reshape(-1), 2), np.tile(np.sin(freqs).reshape(-1), 2)]).astype(np.float32)
    t = np.arange(P)
    lag = t[None, :] - t[:, None]
    decay = np.where((lag >= 0) & (t[None, :] // T == t[:, None] // T), 0.9 ** np.maximum(lag, 0), 0.0)
    part_of = np.concatenate([t[:, None] == np.arange(PARTS), t[:, None] // EXPERTS == np.arange(PARTS)], axis=1)
    return {"rope": rope, "ident": np.eye(P, dtype=np.float32), "decay": decay.astype(np.float32),
            "first": np.arange(EXPERTS, 0, -1).astype(np.float32), "pick_part": part_of.astype(np.float32)}


def kernel(**inputs):
    import numpy as _np
    import concourse.bacc as _bacc
    from concourse import mybir as _mybir
    from concourse.bass_utils import run_bass_kernel_spmd as _run

    nc = _bacc.Bacc("TRN2", target_bir_lowering=False, num_devices=1)
    arrays, args = {}, []
    for name, a in [(n, inputs[n]) for n in _INS] + list(tables().items()):
        a = _np.ascontiguousarray(a)
        arrays[f"in_{name}_dram"] = a
        args.append(nc.dram_tensor(f"in_{name}_dram", a.shape, _mybir.dt.from_np(a.dtype), kind="ExternalInput").ap())
    shape = inputs["x"].shape
    args.append(nc.dram_tensor("out_0_dram", shape, _mybir.dt.float32, kind="ExternalOutput").ap())
    decoder_layer(nc, *args)
    r = _run(nc, [arrays], core_ids=[0])
    return r.results[0]["out_0_dram"]
```

```python
from contextlib import ExitStack

import numpy as np

import concourse.bass as bass
from concourse import mybir

ALU = mybir.AluOpType
ACT = mybir.ActivationFunctionType
F32 = mybir.dt.float32
F16 = mybir.dt.float16
BF16 = mybir.dt.bfloat16
AX_X = mybir.AxisListType.X

P = 128
T = 64
HEADS = 16
DEPTH = 8
QUADS = 4
PAIRS = 8
EXPERTS = 8
HIDDEN = 64
RING = 4
EPS = 1e-5
SCALE = float(DEPTH) ** -0.5
FCOL = DEPTH + 1
VCOL = 2 * 2 * FCOL
M_UNIT = 32.0
PARTS = 3


def decoder_layer(nc, x, ctx_in, w_qkv, b_qkv, w_fc, b_fc, w1, b1, w2, b2, ew, eb, rope, ident, decay, first, pick_part,
                  out):
    tiles = x.shape[0] * x.shape[1] // P
    x_t = x.rearrange("(n b) t d -> (b t) n d", b=2)
    ctx_t = ctx_in.rearrange("(n b) t d -> n (b t) d", b=2)
    out_t = out.rearrange("(n b) t d -> n (b t) d", b=2)

    with ExitStack() as stack:
        def sb(name, shape, dt=F32):
            return stack.enter_context(nc.sbuf_tensor(name, shape, dt))

        def sem(name):
            return stack.enter_context(nc.semaphore(name))

        w_all = sb("w_all", [P, 2, 3 * P])
        w_rot = sb("w_rot", [P, 2, 3 * P])
        b_fc_sb = sb("b_fc_sb", [PARTS, P])
        bv_sb = sb("bv_sb", [P, 1])
        b_out = sb("b_out", [PARTS, P])
        rot = sb("rot", [P, 4, 2, P])
        rope_sb = sb("rope_sb", [P, 2, P])
        part_of = sb("part_of", [P, 2 * PARTS])
        res = sb("res", [PARTS, 2, 3 * P])
        bpart = sb("bpart", [PARTS, PARTS, 3 * P], BF16)
        brow = sb("brow", [PARTS, 2, 3 * P], BF16)
        bias_rows = sb("bias_rows", [PARTS, 3 * P], BF16)
        ones_rows = sb("ones_rows", [PARTS, P], BF16)
        wfc = sb("wfc", [P, P])
        w1_sb = sb("w1_sb", [P, HIDDEN])
        b1_sb = sb("b1_sb", [HIDDEN, 1])
        w2_sb = sb("w2_sb", [HIDDEN, EXPERTS])
        b2_sb = sb("b2_sb", [P, EXPERTS])
        first_sb = sb("first_sb", [P, EXPERTS])
        ew_sb = sb("ew_sb", [P, EXPERTS, P])
        eb_sb = sb("eb_sb", [PARTS * EXPERTS, P])
        eres = sb("eres", [PARTS * EXPERTS, 2, P])
        epart = sb("epart", [PARTS * EXPERTS, PARTS, P], BF16)
        erow = sb("erow", [PARTS * EXPERTS, 4, P], BF16)
        eb_rows = sb("eb_rows", [PARTS * EXPERTS, P], BF16)
        id32 = sb("id32", [P, P])
        id16 = sb("id16", [P, P], F16)
        idb = sb("idb", [P, P], BF16)
        neg_id = sb("neg_id", [P, P], F16)
        decay_sb = sb("decay_sb", [P, P])
        eps_sb = sb("eps_sb", [P, 1])
        half = sb("half", [P, 1])
        zero = sb("zero", [P, 1])

        X = sb("X", [P, tiles, P])
        C = sb("C", [P, RING, P])
        st = sb("st", [P, 3, 2, 6])
        mv = sb("mv", [P, 3, 2, 2])
        ve = sb("ve", [P, 3, 1])
        rstd = sb("rstd", [P, 3, 2, 1])
        mr = sb("mr", [P, 3, 1])
        nmr = sb("nmr", [P, 3, 2, 1])
        xn1 = sb("xn1", [P, 2, P])
        xT = sb("xT", [P, 2, P])
        parts = sb("parts", [P, 2, 2, HEADS, 4, DEPTH], F16)
        qkT = sb("qkT", [P, 2, 2, QUADS, P], F16)
        V = sb("V", [P, RING, 2, PAIRS * VCOL], F16)
        mx = sb("mx", [P, 2, HEADS])
        m16 = sb("m16", [P, 2, HEADS], F16)
        E = sb("E", [P, 2, 2 * 512])
        ET = sb("ET", [P, 2, 2, PAIRS, P], F16)
        rec = sb("rec", [P, HEADS])
        att = sb("att", [P, P])
        attT = sb("attT", [P, P])
        x1 = sb("x1", [P, 2, P])
        kv = sb("kv", [P, 2, P])
        gated = sb("gated", [P, P])
        x2 = sb("x2", [P, RING, P])
        xn3 = sb("xn3", [P, 2, P])
        x3T = sb("x3T", [P, 2, P])
        hT = sb("hT", [HIDDEN, P])
        lg = sb("lg", [P, EXPERTS])
        top = sb("top", [P, 2])
        pick = sb("pick", [P, EXPERTS])
        mask = sb("mask", [P, 2, PARTS, EXPERTS], BF16)
        maskT = sb("maskT", [PARTS * EXPERTS, P], BF16)
        late = sb("late", [P, 4 * P], BF16)
        xm = sb("xm", [P, EXPERTS, P])
        O = sb("O", [P, RING, P])

        ps_s = stack.enter_context(nc.psum_tensor("ps_s", [P, 2, 512], F32))
        ps_t = stack.enter_context(nc.psum_tensor("ps_t", [P, 2, 512], F32))
        ps_p = stack.enter_context(nc.psum_tensor("ps_p", [P, 512], F32))
        ps_q = stack.enter_context(nc.psum_tensor("ps_q", [P, 1024], F16))
        ps_c = stack.enter_context(nc.psum_tensor("ps_c", [P, 512], F32))
        ps_d = stack.enter_context(nc.psum_tensor("ps_d", [P, 512], F32))
        ps_v = ps_q[:, 0:2 * P].bitcast(F32)

        x_in = sem("x_in")
        c_in = [sem(f"c_in{u}") for u in range(RING)]
        o_out = [sem(f"o_out{u}") for u in range(RING)]
        w_ident, w_in_qk, w_in_rope, w_in_b, w_in_fc, w_in_rest, w_in_eb = (sem(n) for n in (
            "w_ident", "w_in_qk", "w_in_rope", "w_in_b", "w_in_fc", "w_in_rest", "w_in_eb"))
        bv_ps = sem("bv_ps")
        made = sem("made")
        v_zero = sem("v_zero")
        eb_made = sem("eb_made")
        id_made = sem("id_made")
        names = ("st1 mv1 ve1 rstd1 mr1 nmr1 xn1 xT_ps xT s_0 s_2 s_1 qk_ps v_ps hi lo_q lo_k dup_q dup_k v_up v_down "
                 "vl_up vl_down qkT_ps qkT s_ps mx m16 sm_ps exp eT_ps eT_a eT_b el_a el_b pv_ps rec_a rec_b att_a "
                 "att_b attT_ps attT kv rs_ps x1 st2 mv2 ve2 rstd2 gated x2 st3 mv3 ve3 rstd3 mr3 nmr3 xn3 x3T_ps x3T "
                 "h_ps hT lg_ps lg top1 pick top2 mask maskT_ps maskT mask_ps late xm xm_late y_ps o").split()
        S = {n: sem("s_" + n) for n in names}

        def done(eng, name, t):
            if isinstance(t, int) and t < 0:
                return
            eng.wait_ge(S[name], t + 1)

        def has(t):
            return not isinstance(t, int) or 0 <= t < tiles

        def steps(eng, step, after_first=None):
            begin, end = 2 * RING, (tiles - 1) // RING * RING
            step(-1, RING - 1)
            if after_first:
                after_first()
            for s in range(0, begin):
                step(s, s % RING)
            with eng.Fori(begin, end, RING) as s0:
                for u in range(RING):
                    step(s0 + u, u)
            for s in range(end, tiles + 6):
                step(s, s % RING)

        def ring_count(t, slot):
            if isinstance(t, int):
                return 16 * (t // RING + 1)
            return (t - slot) * (16 // RING) + 16

        def x_of(t):
            return X[:, bass.ds(t, 1), :].rearrange("p a d -> p (a d)")

        def row(ap):
            return ap.rearrange("(a n) -> a n", a=1)

        def v_views(h2, slot):
            rows = slice(T * h2, T * h2 + T)
            src = ps_v[rows, :].rearrange("p (b g d) -> p b g d", b=2, d=DEPTH)
            return src, [V[rows, slot, part, :].rearrange("p (g b h f) -> p h b g f", b=2, h=2, f=FCOL)[
                :, h2, :, :, 0:DEPTH] for part in range(2)]

        V_ZERO = 1 + 2 * RING + 4
        EB_MADE = 10
        MADE_QKV = 4 + 2 + 2
        MADE_IN = MADE_QKV + 8
        MADE_OUT = MADE_IN + 1 + 8

        block = stack.enter_context(nc.Block())

        @block.sync
        def _(sp):
            def step(s, u):
                n, o = s + 1, s - 6
                if has(n) and not (isinstance(n, int) and n < RING):
                    done(sp, "kv", n - RING)
                    sp.dma_start(C[:, (u + 1) % RING, :], ctx_t[bass.ds(n, 1)].rearrange("a p d -> p (a d)")).then_inc(
                        c_in[(u + 1) % RING], 16)
                if has(o):
                    done(sp, "o", o)
                    sp.dma_start(out_t[bass.ds(o, 1)].rearrange("a p d -> p (a d)"), O[:, (u - 6) % RING, :]).then_inc(
                        o_out[(u - 6) % RING], 16)

            sp.dma_start(w_all[:, 0, :], w_qkv).then_inc(w_in_qk, 16)
            sp.dma_start(X[:, 0:RING, :], x_t[:, 0:RING, :]).then_inc(x_in, 16)
            sp.dma_start(part_of[:, :], pick_part).then_inc(w_in_b, 16)
            fc_rows = w_fc.rearrange("(g j d) n -> j g d n", j=4, d=DEPTH)
            bv_rows = b_qkv[2 * P:3 * P].rearrange("(g j d a) -> j g d a", j=4, d=DEPTH, a=1)
            for j in range(4):
                sp.dma_start(wfc[32 * j:32 * j + 32, :], fc_rows[j]).then_inc(w_in_fc, 16)
                sp.dma_start(bv_sb[32 * j:32 * j + 32, :], bv_rows[j]).then_inc(w_in_fc, 16)
            sp.dma_start(b_fc_sb[:, :], row(b_fc).to_broadcast([PARTS, P])).then_inc(w_in_fc, 16)
            sp.dma_start(decay_sb[:, :], decay).then_inc(w_in_rest, 16)
            for t in range(RING):
                sp.dma_start(C[:, t, :], ctx_t[t]).then_inc(c_in[t], 16)
            for dst, src in ((w1_sb[:, :], w1), (b1_sb[:, :], b1.rearrange("(n a) -> n a", a=1)), (w2_sb[:, :], w2),
                             (b2_sb[:, :], row(b2).to_broadcast([P, EXPERTS])),
                             (first_sb[:, :], row(first).to_broadcast([P, EXPERTS])),
                             (ew_sb[:, :, :], ew.rearrange("e k n -> k e n"))):
                sp.dma_start(dst, src).then_inc(w_in_rest, 16)
            for c in range(PARTS):
                sp.dma_start(eb_sb[EXPERTS * c:EXPERTS * c + EXPERTS, :], eb).then_inc(w_in_eb, 16)
            for n in range(1, tiles // RING):
                sp.wait_ge(x_in, 16 * n)
                sp.dma_start(X[:, RING * n:RING * n + RING, :], x_t[:, RING * n:RING * n + RING, :]).then_inc(x_in, 16)
            steps(sp, step)
            for u in range(RING):
                sp.wait_ge(o_out[u], 16 * (tiles // RING))

        @block.gpsimd
        def _(pool):
            g = nc.gpsimd
            count = 0

            def link(ins, counter):
                nonlocal count
                count += 1
                ins.then_inc(counter, 1)
                pool.wait_ge(counter, count)

            g.memset(eps_sb[:, :], EPS).then_inc(v_zero, 1)
            g.memset(half[:, :], -0.5).then_inc(v_zero, 1)
            g.memset(zero[:, :], 0.0).then_inc(v_zero, 1)
            g.memset(ones_rows[:, :], 1.0).then_inc(v_zero, 1)
            count = 4
            link(g.memset(V[:, :, :, :].rearrange("p r c n -> p (r c n)").bitcast(F32), 0.0), v_zero)
            for h2 in range(2):
                for r in range(RING):
                    ones = V[T * h2:T * h2 + T, r, 0, :].rearrange("p (g b h f) -> p g b h f", b=2, h=2, f=FCOL)
                    g.memset(ones[:, :, :, h2, DEPTH], 1.0).then_inc(v_zero, 1)

            def root(n, t, p):
                done(pool, f"mv{n}", t)
                g.tensor_tensor(ve[:, n - 1, :], mv[:, n - 1, p, 1:2], eps_sb[:, :], ALU.add).then_inc(S[f"ve{n}"], 1)
                done(pool, f"ve{n}", t)
                g.tensor_tensor(rstd[:, n - 1, p, :], ve[:, n - 1, :], half[:, :], ALU.pow).then_inc(S[f"rstd{n}"], 1)
                if n != 2:
                    done(pool, f"rstd{n}", t)
                    g.tensor_tensor(mr[:, n - 1, :], mv[:, n - 1, p, 0:1], rstd[:, n - 1, p, :],
                                    ALU.mult).then_inc(S[f"mr{n}"], 1)
                    done(pool, f"mr{n}", t)
                    g.tensor_tensor(nmr[:, n - 1, p, :], zero[:, :], mr[:, n - 1, :],
                                    ALU.subtract).then_inc(S[f"nmr{n}"], 1)

            def split_eb():
                nonlocal count
                count = 0
                pool.wait_ge(w_in_eb, 16 * PARTS)
                link(g.tensor_copy(epart[:, 0, :], eb_sb[:, :]), eb_made)
                link(g.tensor_tensor(eres[:, 0, :], eb_sb[:, :], epart[:, 0, :], ALU.subtract), eb_made)
                link(g.tensor_copy(epart[:, 1, :], eres[:, 0, :]), eb_made)
                link(g.tensor_tensor(eres[:, 1, :], eres[:, 0, :], epart[:, 1, :], ALU.subtract), eb_made)
                link(g.tensor_copy(epart[:, 2, :], eres[:, 1, :]), eb_made)

            def place_eb():
                pool.wait_ge(w_in_b, 16)
                for c in range(PARTS):
                    mine = part_of[0:PARTS * EXPERTS, PARTS + c:PARTS + c + 1]
                    link(g.tensor_scalar(erow[:, c, :], epart[:, c, :], mine, None, ALU.mult), eb_made)
                link(g.tensor_tensor(erow[:, 3, :], erow[:, 0, :], erow[:, 1, :], ALU.add), eb_made)
                link(g.tensor_tensor(eb_rows[:, :], erow[:, 3, :], erow[:, 2, :], ALU.add), eb_made)
                assert count == EB_MADE

            def step(s, u):
                z, c, r, e = s + 1, s - 3, s - 4, s - 5
                odd, even = (u + 1) % 2, u % 2
                if has(c):
                    pool.wait_ge(c_in[(u - 3) % RING], ring_count(c, (u - 3) % RING))
                    cc = C[:, (u - 3) % RING, :]
                    g.tensor_tensor(kv[:, odd, :], cc, cc, ALU.mult).then_inc(S["kv"], 1)
                if has(r):
                    root(3, r, even)
                if has(z):
                    root(1, z, odd)
                if has(e):
                    done(pool, "late", e)
                    g.tensor_tensor(xm[:, 4:, :], x3T[:, odd, :].unsqueeze(1).to_broadcast([P, 4, P]),
                                    late[:, :].rearrange("p (e t) -> p e t", t=P), ALU.mult).then_inc(S["xm_late"], 1)
                if has(c):
                    root(2, c, odd)
                if isinstance(s, int) and s == 1:
                    split_eb()
                if isinstance(s, int) and s == 2:
                    place_eb()

            pool.wait_ge(v_zero, V_ZERO)
            steps(pool, step)

        @block.vector
        def _(dve):
            v = nc.vector
            count = 0

            def link(ins):
                nonlocal count
                count += 1
                ins.then_inc(made, 1)
                dve.wait_ge(made, count)

            def split_bias(src, cols):
                nonlocal count
                link(v.tensor_copy(bpart[:, 0, cols], src))
                link(v.tensor_tensor(res[:, 0, cols], src, bpart[:, 0, cols], ALU.subtract))
                count += 1
                v.tensor_scalar(brow[:, 0, cols], bpart[:, 0, cols], part_of[0:PARTS, 0:1], None,
                                ALU.mult).then_inc(made, 1)
                link(v.tensor_copy(bpart[:, 1, cols], res[:, 0, cols]))
                link(v.tensor_tensor(res[:, 1, cols], res[:, 0, cols], bpart[:, 1, cols], ALU.subtract))
                count += 1
                v.scalar_tensor_tensor(out=brow[:, 1, cols], in0=bpart[:, 1, cols], scalar=part_of[0:PARTS, 1:2],
                                       in1=brow[:, 0, cols], op0=ALU.mult, op1=ALU.add).then_inc(made, 1)
                link(v.tensor_copy(bpart[:, 2, cols], res[:, 1, cols]))
                link(v.scalar_tensor_tensor(out=bias_rows[:, cols], in0=bpart[:, 2, cols], scalar=part_of[0:PARTS, 2:3],
                                            in1=brow[:, 1, cols], op0=ALU.mult, op1=ALU.add))

            def setup_in():
                nonlocal count
                dve.wait_ge(w_in_qk, 32)
                dve.wait_ge(w_in_rope, 16)
                src = w_all[:, :, 0:2 * P].rearrange("p b (m e) -> p b e m", e=2)
                dst = w_rot[:, :, 0:2 * P].rearrange("p b (m e) -> p b e m", e=2)
                for q, (e, cs) in enumerate(((0, 0), (1, 1), (0, 1), (1, 0))):
                    v.tensor_tensor(rot[:, q, :, :], src[:, :, e, :],
                                    rope_sb[:, cs, :].unsqueeze(1).to_broadcast([P, 2, P]), ALU.mult).then_inc(made, 1)
                for h2 in range(2):
                    s_ = w_all[:, 0, 2 * P:].rearrange("p (g h j d) -> p h j g d", g=2, h=2, j=4)[:, h2]
                    d_ = w_rot[:, 0, 2 * P:3 * P].rearrange("p (h j g d) -> p h j g d", g=2, h=2, j=4)[:, h2]
                    count = 5
                    if h2 == 0:
                        v.tensor_copy(d_, s_).then_inc(made, 1)
                    else:
                        link(v.tensor_copy(d_, s_))
                v.tensor_tensor(dst[:, :, 0, :], rot[:, 0], rot[:, 1], ALU.subtract).then_inc(made, 1)
                count = MADE_QKV - 1
                link(v.tensor_tensor(dst[:, :, 1, :], rot[:, 2], rot[:, 3], ALU.add))
                dve.wait_ge(w_in_b, 16)
                split_bias(w_rot[0:PARTS, 1, 0:2 * P], slice(0, 2 * P))
                assert count == MADE_IN, count

            def setup_out():
                dve.wait_ge(bv_ps, 1)
                link(v.tensor_tensor(b_out[:, :], ps_c[0:PARTS, 0:P], b_fc_sb[:, :], ALU.add))
                split_bias(b_out[:, :], slice(2 * P, 3 * P))
                assert count == MADE_OUT, count

            def step(s, u):
                z, a, b, p, c, r, e, o = s + 1, s, s - 1, s - 2, s - 3, s - 4, s - 5, s - 6
                odd, even = (u + 1) % 2, u % 2

                def low_exp(name, k):
                    v.tensor_tensor(ET[:, even, 1, 4 * k:4 * k + 4, :].rearrange("p g t -> p (g t)"), ps_t[:, k, :],
                                    ET[:, even, 0, 4 * k:4 * k + 4, :].rearrange("p g t -> p (g t)"),
                                    ALU.subtract).then_inc(S[name], 1)

                def low_qk(name, qk):
                    mine = parts[:, even, qk]
                    v.tensor_tensor(mine[:, :, 2 - qk, :], ps_p[:, P * qk:P * qk + P].rearrange("p (h d) -> p h d", d=DEPTH),
                                    mine[:, :, 0, :], ALU.subtract).then_inc(S[name], 1)

                def low_v(name, h2):
                    src, (v_hi, v_lo) = v_views(h2, u)
                    v.tensor_tensor(v_lo, src, v_hi, ALU.subtract).then_inc(S[name], 1)

                def divide(sums, name, t, lo, hi, got, over):
                    done(dve, sums, t)
                    v.tensor_tensor(att[lo:hi, :].rearrange("p (g h f) -> p g h f", h=2, f=DEPTH),
                                    got[:, :, :, 0:DEPTH], over.unsqueeze(3).to_broadcast([T, PAIRS, 2, DEPTH]),
                                    ALU.mult).then_inc(S[name], 1)

                if has(z):
                    if u == RING - 1:
                        dve.wait_ge(x_in, ring_count(z, 0))
                        dve.nop(nofuse=True)
                    v.bn_stats(st[:, 0, odd, :], x_of(z)).then_inc(S["st1"], 1)
                if has(p):
                    done(dve, "eT_a", p)
                    low_exp("el_a", 0)
                if has(o):
                    slot = (u - 6) % RING
                    done(dve, "y_ps", o)
                    if not (isinstance(o, int) and o < RING):
                        dve.wait_ge(o_out[slot], ring_count(o - RING, slot))
                    v.tensor_tensor(O[:, slot, :], ps_d[:, 0:P], x2[:, slot, :], ALU.add).then_inc(S["o"], 1)
                if has(p):
                    done(dve, "eT_b", p)
                    low_exp("el_b", 1)
                if has(b):
                    if has(z):
                        done(dve, "st1", z)
                    done(dve, "s_ps", b)
                    v.tensor_reduce(mx[:, odd, :], ps_s[:, :, :].rearrange("p k (h t) -> p (k h) t", t=T), AX_X,
                                    ALU.max).then_inc(S["mx"], 1)
                if has(z):
                    if isinstance(s, int):
                        done(dve, "st1", z)
                    v.bn_aggr(mv[:, 0, odd, :], st[:, 0, odd, :]).then_inc(S["mv1"], 1)
                if has(c):
                    done(dve, "rs_ps", c)
                    v.tensor_tensor(x1[:, odd, :], ps_c[:, P:2 * P], x_of(c), ALU.add).then_inc(S["x1"], 1)
                if has(b):
                    done(dve, "mx", b)
                    v.tensor_scalar(m16[:, odd, :], mx[:, odd, :], 1.0 / M_UNIT, None, ALU.mult).then_inc(S["m16"], 1)
                if has(a):
                    done(dve, "hi", a)
                    low_qk("lo_q", 0)
                    low_qk("lo_k", 1)
                if has(c):
                    done(dve, "x1", c)
                    v.bn_stats(st[:, 1, odd, :], x1[:, odd, :]).then_inc(S["st2"], 1)
                if has(a):
                    done(dve, "lo_q", a)
                    pairs = parts[:, even, 0].rearrange("p h (a c) d -> p h c a d", c=2)
                    v.tensor_copy(pairs[:, :, 1], pairs[:, :, 0]).then_inc(S["dup_q"], 1)
                if has(a):
                    if has(c):
                        done(dve, "st2", c)
                    done(dve, "v_up", a)
                    low_v("vl_up", 0)
                if has(c):
                    if isinstance(s, int):
                        done(dve, "st2", c)
                    v.bn_aggr(mv[:, 1, odd, :], st[:, 1, odd, :]).then_inc(S["mv2"], 1)
                if has(a):
                    done(dve, "lo_k", a)
                    v.tensor_copy(parts[:, even, 1, :, 2:4, :], parts[:, even, 1, :, 0:2, :]).then_inc(S["dup_k"], 1)
                if has(a):
                    done(dve, "v_down", a)
                    low_v("vl_down", 1)
                if has(e):
                    done(dve, "mask_ps", e)
                    done(dve, "x3T", e)
                    v.tensor_tensor(xm[:, 0:4, :], x3T[:, odd, :].unsqueeze(1).to_broadcast([P, 4, P]),
                                    ps_t[:, 0, :].rearrange("p (e t) -> p e t", t=P), ALU.mult).then_inc(S["xm"], 1)
                if has(r):
                    done(dve, "lg_ps", r)
                    v.tensor_tensor(lg[:, :], ps_d[:, 384:384 + EXPERTS], b2_sb[:, :], ALU.add).then_inc(S["lg"], 1)
                if has(c):
                    done(dve, "mv2", c)
                    v.scalar_tensor_tensor(out=gated[:, :], in0=x1[:, odd, :], scalar=mv[:, 1, odd, 0:1],
                                           in1=ps_c[:, 2 * P:3 * P], op0=ALU.subtract,
                                           op1=ALU.mult).then_inc(S["gated"], 1)
                halves = []
                if has(p):
                    done(dve, "pv_ps", p)
                    for b_ in range(2):
                        lo, hi = T * b_, T * b_ + T
                        got = ps_p[lo:hi, 0:PAIRS * VCOL].rearrange("p (g b h f) -> p b g h f", b=2, h=2, f=FCOL)[:, b_]
                        over = rec[lo:hi, :].rearrange("p (g h) -> p g h", h=2)
                        v.reciprocal(over, got[:, :, :, DEPTH]).then_inc(S["rec_a" if b_ == 0 else "rec_b"], 1)
                        halves.append((lo, hi, got, over))
                if has(r):
                    done(dve, "lg", r)
                    v.tensor_reduce(top[:, 0:1], lg[:, :], AX_X, ALU.max).then_inc(S["top1"], 1)
                if has(c):
                    done(dve, "gated", c)
                    done(dve, "rstd2", c)
                    v.scalar_tensor_tensor(out=x2[:, (u - 3) % RING, :], in0=gated[:, :], scalar=rstd[:, 1, odd, :],
                                           in1=x1[:, odd, :], op0=ALU.mult, op1=ALU.add).then_inc(S["x2"], 1)
                if has(r):
                    done(dve, "top1", r)
                    v.scalar_tensor_tensor(out=pick[:, :], in0=lg[:, :], scalar=top[:, 0:1], in1=first_sb[:, :],
                                           op0=ALU.is_ge, op1=ALU.mult).then_inc(S["pick"], 1)
                if has(c):
                    done(dve, "x2", c)
                    v.bn_stats(st[:, 2, odd, :], x2[:, (u - 3) % RING, :]).then_inc(S["st3"], 1)
                if has(p):
                    divide("rec_a", "att_a", p, *halves[0])
                if has(r):
                    if has(c):
                        done(dve, "st3", c)
                    done(dve, "pick", r)
                    v.tensor_reduce(top[:, 1:2], pick[:, :], AX_X, ALU.max).then_inc(S["top2"], 1)
                if has(c):
                    if isinstance(s, int):
                        done(dve, "st3", c)
                    v.bn_aggr(mv[:, 2, odd, :], st[:, 2, odd, :]).then_inc(S["mv3"], 1)
                if has(p):
                    divide("rec_b", "att_b", p, *halves[1])
                if has(r):
                    done(dve, "top2", r)
                    v.tensor_scalar(mask[:, even, :, :], pick[:, :].unsqueeze(1).to_broadcast([P, PARTS, EXPERTS]),
                                    top[:, 1:2], None, ALU.is_equal).then_inc(S["mask"], 1)
                if isinstance(s, int) and s == 1:
                    setup_out()

            steps(dve, step, setup_in)

        @block.scalar
        def _(act):
            sc = nc.scalar
            act.dma_start(rope_sb[:, :, :], rope.rearrange("(a c) n -> a c n", a=1).to_broadcast([P, 2, P])).then_inc(
                w_in_rope, 16)
            act.dma_start(w_all[:, 1, 0:2 * P], row(b_qkv[0:2 * P]).to_broadcast([P, 2 * P])).then_inc(w_in_qk, 16)
            act.dma_start(id32[:, :], ident).then_inc(w_ident, 16)
            act.wait_ge(w_ident, 16)
            sc.copy(id16[:, :], id32[:, :]).then_inc(id_made, 1)
            sc.copy(idb[:, :], id32[:, :]).then_inc(id_made, 1)
            sc.mul(neg_id[:, :], id32[:, :], -M_UNIT).then_inc(id_made, 1)

            def step(s, u):
                z, a, b, p, c, r, e = s + 1, s, s - 1, s - 2, s - 3, s - 4, s - 5
                odd, even = (u + 1) % 2, u % 2
                if has(p):
                    done(act, "eT_ps", p)
                    for k, name in enumerate(("eT_a", "eT_b")):
                        sc.copy(ET[:, even, 0, 4 * k:4 * k + 4, :].rearrange("p g t -> p (g t)"),
                                ps_t[:, k, :]).then_inc(S[name], 1)
                if has(a):
                    done(act, "xT_ps", a)
                    sc.copy(xT[:, even, :], ps_p[:, 0:P]).then_inc(S["xT"], 1)
                if has(c):
                    done(act, "attT_ps", c)
                    sc.copy(attT[:, :], ps_c[:, 0:P]).then_inc(S["attT"], 1)
                if has(r):
                    done(act, "nmr3", r)
                    act.nop(nofuse=True)
                    sc.activation(xn3[:, even, :], x2[:, (u - 4) % RING, :], ACT.Identity, scale=rstd[:, 2, even, :],
                                  bias=nmr[:, 2, even, :]).then_inc(S["xn3"], 1)
                if has(a):
                    done(act, "qk_ps", a)
                    sc.copy(parts[:, even, :, :, 0, :].rearrange("p q h d -> p (q h) d"),
                            ps_p[:, 0:2 * P].rearrange("p (h d) -> p h d", d=DEPTH)).then_inc(S["hi"], 1)
                if has(e):
                    done(act, "maskT_ps", e)
                    if has(r):
                        done(act, "x3T_ps", r)
                    sc.copy(maskT[:, :], ps_d[0:PARTS * EXPERTS, 448:512].bitcast(BF16)).then_inc(S["maskT"], 1)
                if has(r):
                    done(act, "x3T_ps", r)
                    sc.copy(x3T[:, even, :], ps_d[:, P:2 * P]).then_inc(S["x3T"], 1)
                if has(a):
                    done(act, "v_ps", a)
                    for h2, name in ((0, "v_up"), (1, "v_down")):
                        src, (v_hi, _) = v_views(h2, u)
                        sc.copy(v_hi, src).then_inc(S[name], 1)
                if has(e):
                    done(act, "mask_ps", e)
                    sc.copy(late[:, :], ps_t[:, 1, :]).then_inc(S["late"], 1)
                if has(r):
                    done(act, "h_ps", r)
                    sc.activation(hT[:, :], ps_d[0:HIDDEN, 2 * P:3 * P], ACT.Relu, bias=b1_sb[:, :]).then_inc(S["hT"], 1)
                if has(b):
                    done(act, "sm_ps", b)
                    sc.activation(E[:, odd, :], ps_s[:, :, :].rearrange("p k n -> p (k n)"), ACT.Exp,
                                  scale=SCALE).then_inc(S["exp"], 1)
                if has(z):
                    done(act, "nmr1", z)
                    act.nop(nofuse=True)
                    sc.activation(xn1[:, odd, :], x_of(z), ACT.Identity, scale=rstd[:, 0, odd, :],
                                  bias=nmr[:, 0, odd, :]).then_inc(S["xn1"], 1)
                if has(a):
                    done(act, "qkT_ps", a)
                    sc.copy(qkT[:, even, :, :, :].rearrange("p q g t -> p (q g t)"), ps_q[:, :]).then_inc(S["qkT"], 1)

            steps(act, step)

        @block.tensor
        def _(pe):
            mm = nc.tensor.matmul

            def step(s, u):
                a, b, p, c, r, e = s, s - 1, s - 2, s - 3, s - 4, s - 5
                odd, even = (u + 1) % 2, u % 2
                if has(a):
                    done(pe, "xn1", a)
                    done(pe, "att_b", a - 3)
                    nc.tensor.transpose(ps_p[:, 0:P], xn1[:, even, :], id32[:, :]).then_inc(S["xT_ps"], 1)
                if has(c):
                    done(pe, "att_b", c)
                    done(pe, "gated", c - 1)
                    nc.tensor.transpose(ps_c[:, 0:P], att[:, :], id32[:, :]).then_inc(S["attT_ps"], 1)
                if has(b):
                    done(pe, "qkT", b)
                    for j in (0, 2, 1, 3):
                        rows = slice(32 * j, 32 * j + 32)
                        if j % 2:
                            done(pe, f"s_{j - 1}", b)
                        for g in range(QUADS):
                            for b_ in range(2):
                                t = slice(T * b_, T * b_ + T)
                                at = 256 * (j % 2) + 64 * g
                                last = mm(ps_s[t, j // 2, at:at + T], qkT[rows, odd, 0, g, t], qkT[rows, odd, 1, g, t],
                                          start=(j in (0, 2) and g == 0), stop=False, skip_group_check=True)
                        if j < 3:
                            last.then_inc(S[f"s_{j}"], 1)
                    last.then_inc(S["s_ps"], 1)
                if has(a):
                    if isinstance(a, int) and a == 0:
                        pe.wait_ge(v_zero, V_ZERO)
                        pe.wait_ge(made, MADE_QKV)
                    done(pe, "xT", a)
                    mm(ps_p[:, 0:2 * P], xT[:, even, :], w_rot[:, 0, 0:2 * P], start=True, stop=False)
                    if isinstance(a, int) and a == 0:
                        pe.wait_ge(made, MADE_IN)
                    mm(ps_p[:, 0:2 * P], ones_rows[:, :], bias_rows[:, 0:2 * P], start=False,
                       stop=True).then_inc(S["qk_ps"], 1)
                if isinstance(s, int) and s == 0:
                    pe.wait_ge(w_in_fc, 16 * 9)
                    mm(ps_c[0:PARTS, 0:P], bv_sb[:, :].to_broadcast([P, PARTS]), wfc[:, :], start=True,
                       stop=True).then_inc(bv_ps, 1)
                if has(c):
                    if isinstance(c, int) and c == 0:
                        pe.wait_ge(made, MADE_OUT)
                        pe.wait_ge(w_in_rest, 16 * 7)
                    done(pe, "attT", c)
                    mm(ps_c[:, P:2 * P], attT[:, :], wfc[:, :], start=True, stop=False)
                    mm(ps_c[:, P:2 * P], ones_rows[:, :], bias_rows[:, 2 * P:3 * P], start=False, stop=True)
                    done(pe, "kv", c)
                    mm(ps_c[:, 2 * P:3 * P], decay_sb[:, :], kv[:, odd, :], start=True, stop=True).then_inc(S["rs_ps"], 1)
                if has(e):
                    done(pe, "mask", e)
                    done(pe, "o", e - 1)
                    nc.tensor.transpose(ps_d[0:PARTS * EXPERTS, 448:512].bitcast(BF16),
                                        mask[:, odd].rearrange("p c e -> p (c e)"), idb[:, :]).then_inc(S["maskT_ps"], 1)
                if has(r):
                    done(pe, "xn3", r)
                    nc.tensor.transpose(ps_d[:, P:2 * P], xn3[:, even, :], id32[:, :]).then_inc(S["x3T_ps"], 1)
                if has(a):
                    done(pe, "xT", a)
                    for b_ in range(2):
                        for h2 in range(2):
                            dst = ps_v[T * h2:T * h2 + T, T * b_:T * b_ + T]
                            cols = slice(2 * P + T * h2, 2 * P + T * h2 + T)
                            last = mm(dst, xT[:, even, T * b_:T * b_ + T], w_rot[:, 0, cols], start=True, stop=True)
                    last.then_inc(S["v_ps"], 1)
                if has(e):
                    done(pe, "mask", e)
                    if has(p):
                        done(pe, "el_b", p)
                    for x_ in range(EXPERTS):
                        last = mm(ps_t[:, x_ // 4, P * (x_ % 4):P * (x_ % 4) + P],
                                  mask[:, odd, 0, x_:x_ + 1].to_broadcast([P, P]), idb[:, :], start=True, stop=True)
                    last.then_inc(S["mask_ps"], 1)
                if has(r):
                    done(pe, "x3T", r)
                    if has(e):
                        done(pe, "maskT", e)
                    mm(ps_d[0:HIDDEN, 2 * P:3 * P], w1_sb[:, :], x3T[:, even, :], start=True,
                       stop=True).then_inc(S["h_ps"], 1)
                if has(b):
                    done(pe, "m16", b)
                    for k in range(2):
                        last = mm(ps_s[:, k, :], neg_id[:, :],
                                  m16[:, odd, 8 * k:8 * k + 8].unsqueeze(2).to_broadcast([P, 8, T]), start=False,
                                  stop=True, skip_group_check=True)
                    last.then_inc(S["sm_ps"], 1)
                if has(p):
                    done(pe, "el_b", p)
                    if has(a):
                        done(pe, "lo_k", a)
                    slot = (u - 2) % RING
                    for g in range(PAIRS):
                        cols = slice(VCOL * g, VCOL * g + VCOL)
                        mm(ps_p[:, cols], ET[:, even, 0, g, :], V[:, slot, 0, cols], start=True, stop=False)
                        mm(ps_p[:, cols], ET[:, even, 0, g, :], V[:, slot, 1, cols], start=False, stop=False)
                        last = mm(ps_p[:, cols], ET[:, even, 1, g, :], V[:, slot, 0, cols], start=False, stop=True)
                    last.then_inc(S["pv_ps"], 1)
                if has(r):
                    done(pe, "hT", r)
                    mm(ps_d[:, 384:384 + EXPERTS], hT[:, :], w2_sb[:, :], start=True, stop=True).then_inc(S["lg_ps"], 1)
                if has(a):
                    done(pe, "dup_k", a)
                    done(pe, "vl_down", a)
                    for qk in range(2):
                        for g in range(QUADS):
                            at = P * (QUADS * qk + g)
                            src = parts[:, even, qk, 4 * g:4 * g + 4, :, :].rearrange("p h a d -> p (h a d)")
                            last = nc.tensor.transpose(ps_q[:, at:at + P], src, id16[:, :])
                    last.then_inc(S["qkT_ps"], 1)
                if has(e):
                    done(pe, "xm", e)
                    if isinstance(e, int) and e == 0:
                        pe.wait_ge(eb_made, EB_MADE)
                    if has(r):
                        done(pe, "lg", r)
                    done(pe, "maskT", e)
                    for x_ in range(EXPERTS // 2):
                        mm(ps_d[:, 0:P], xm[:, x_, :], ew_sb[:, x_, :], start=(x_ == 0), stop=False)
                if has(b):
                    done(pe, "exp", b)
                    done(pe, "xm", e)
                    done(pe, "late", e)
                    for g in range(PAIRS):
                        last = nc.tensor.transpose(ps_t[:, g // 4, P * (g % 4):P * (g % 4) + P],
                                                   E[:, odd, P * g:P * g + P], id32[:, :])
                    last.then_inc(S["eT_ps"], 1)
                if has(e):
                    done(pe, "xm_late", e)
                    for x_ in range(EXPERTS // 2, EXPERTS):
                        mm(ps_d[:, 0:P], xm[:, x_, :], ew_sb[:, x_, :], start=False, stop=False)
                    mm(ps_d[:, 0:P], maskT[:, :], eb_rows[:, :], start=False, stop=True).then_inc(S["y_ps"], 1)

            pe.wait_ge(w_ident, 16)
            pe.wait_ge(id_made, 3)
            steps(pe, step)


_INS = ["x", "ctx_1024", "L0_attn_w_qkv", "L0_attn_b_qkv", "L0_attn_w_fc", "L0_attn_b_fc", "L0_ffn_W1", "L0_ffn_b1",
        "L0_ffn_W2", "L0_ffn_b2", "L0_ffn_expert_W", "L0_ffn_expert_b"]


def tables():
    inv_freq = (1.0 / 10000.0 ** (np.arange(0, DEPTH, 2, dtype=np.float32) / DEPTH)).astype(np.float32)
    freqs = np.arange(HEADS, dtype=np.float32)[:, None] * inv_freq[None, :]
    rope = np.stack([np.tile(np.cos(freqs).reshape(-1), 2), np.tile(np.sin(freqs).reshape(-1), 2)]).astype(np.float32)
    t = np.arange(P)
    lag = t[None, :] - t[:, None]
    decay = np.where((lag >= 0) & (t[None, :] // T == t[:, None] // T), 0.9 ** np.maximum(lag, 0), 0.0)
    part_of = np.concatenate([t[:, None] == np.arange(PARTS), t[:, None] // EXPERTS == np.arange(PARTS)], axis=1)
    return {"rope": rope, "ident": np.eye(P, dtype=np.float32), "decay": decay.astype(np.float32),
            "first": np.arange(EXPERTS, 0, -1).astype(np.float32), "pick_part": part_of.astype(np.float32)}


def kernel(**inputs):
    import numpy as _np
    import concourse.bacc as _bacc
    from concourse import mybir as _mybir
    from concourse.bass_utils import run_bass_kernel_spmd as _run

    nc = _bacc.Bacc("TRN2", target_bir_lowering=False, num_devices=1)
    arrays, args = {}, []
    for name, a in [(n, inputs[n]) for n in _INS] + list(tables().items()):
        a = _np.ascontiguousarray(a)
        arrays[f"in_{name}_dram"] = a
        args.append(nc.dram_tensor(f"in_{name}_dram", a.shape, _mybir.dt.from_np(a.dtype), kind="ExternalInput").ap())
    shape = inputs["x"].shape
    args.append(nc.dram_tensor("out_0_dram", shape, _mybir.dt.float32, kind="ExternalOutput").ap())
    decoder_layer(nc, *args)
    r = _run(nc, [arrays], core_ids=[0])
    return r.results[0]["out_0_dram"]
```
